# Optimizing a Trainium2 kernel written in Bass

```python
import numpy as np
import jax
import jax.numpy as jnp

def _softmax(x, axis=-1):
    return jax.nn.softmax(x, axis=axis)

def _gelu(x):
    return jax.nn.gelu(x, approximate=True)

def _silu(x):
    return jax.nn.silu(x)

def _sigmoid(x):
    return jax.nn.sigmoid(x)

def _layernorm(x, axis=-1, eps=1e-05):
    m = jnp.mean(x, axis=axis, keepdims=True)
    v = jnp.var(x, axis=axis, keepdims=True)
    return (x - m) / jnp.sqrt(v + eps)

def _scatter_add(tgt, idx, src, axis=0):
    return tgt.at[idx].add(src)

def _segment_sum(src, seg, n):
    return jax.ops.segment_sum(src, seg, n)
kernel_name = 'mk_adj_preln_d2_adj_r2_8a24e9'

def setup_inputs(seed: int=0):
    np.random.seed(seed)
    _w = jnp.asarray

    def _rec_inputs():
        import jax
        import jax.numpy as jnp
        _gk = jax.random.key(seed)
        x = -0.0002928 + 1 * jax.random.normal(jax.random.fold_in(_gk, 1), (2048, 256), jnp.float32)
        _w = (1.0 + jnp.arange(2048, dtype=jnp.float32)) ** (-0.5)
        _w = _w / _w.mean()
        _pij = jnp.clip(0.00195312 * _w[:, None] * _w[None, :], 0.0, 1.0)
        _a = jax.random.uniform(jax.random.fold_in(_gk, 2), (2048, 2048)) < _pij
        _a = jnp.logical_or(_a, jnp.swapaxes(_a, -1, -2))
        _a = jnp.logical_or(_a, jnp.eye(2048, dtype=bool))
        _af = _a.astype(jnp.float32)
        _af = _af * jax.random.uniform(jax.random.fold_in(_gk, 3), (2048, 2048), jnp.float32, 0.05, 5.41998)
        adj = _af
        return (x, adj)
    x, adj = _rec_inputs()

    def _L0_gnn_setup():
        import jax, jax.numpy as jnp
        import numpy as np
        N = 4096
        D = 256
        key = jax.random.key(seed)
        ks = jax.random.split(key, 6)
        s = 1.0 / np.sqrt(D)
        return {'x': jax.random.normal(ks[0], (N, D), jnp.float32), 'spatial_encoding': jax.random.normal(ks[1], (N, N), jnp.float32), 'edge_encoding': jax.random.normal(ks[2], (N, N), jnp.float32), 'Wq': jax.random.normal(ks[3], (D, D), jnp.float32) * s, 'bq': jnp.zeros((D,), jnp.float32), 'Wk': jax.random.normal(ks[4], (D, D), jnp.float32) * s, 'bk': jnp.zeros((D,), jnp.float32), 'Wv': jax.random.normal(ks[5], (D, D), jnp.float32) * s, 'bv': jnp.zeros((D,), jnp.float32)}
    _L0_gnn_all = _L0_gnn_setup()
    _L0_gnn_in = {k: v for k, v in _L0_gnn_all.items() if k in ('Wq', 'bq', 'Wk', 'bk', 'Wv', 'bv')}
    del _L0_gnn_all

    def _L1_gnn_setup():
        import jax, jax.numpy as jnp
        import numpy as np
        N, F, H = (1536, 256, 4)
        D = F // H
        ALPHA = 0.5
        EPS = 1e-06

        def _batchnorm(x, gamma, beta):
            m = jnp.mean(x, axis=0)
            v = jnp.var(x, axis=0)
            return (x - m) * jax.lax.rsqrt(v + EPS) * gamma + beta

        def _masked_softmax(scores, mask):
            s = jnp.where(mask, scores, -jnp.inf)
            att = jax.nn.softmax(s, axis=-1)
            return jnp.where(mask, att, 0.0)

        def _mlp_block(x, Wm, bm, g, b):
            h = jax.nn.elu(x @ Wm.T + bm) + x
            return _batchnorm(h, g, b)
        key = jax.random.key(seed)
        ks = jax.random.split(key, 12)
        X = jax.random.normal(ks[0], (N, F), dtype=jnp.float32)
        eye = jnp.eye(N, dtype=jnp.float32)
        local = (jax.random.uniform(ks[1], (N, N)) < 32.0 / N).astype(jnp.float32)
        local = jnp.clip(local + eye, 0.0, 1.0)
        longr = (jax.random.uniform(ks[2], (N, N)) < 16.0 / N).astype(jnp.float32)
        longr = jnp.clip(longr + eye, 0.0, 1.0)
        W = jax.random.normal(ks[3], (H, D, D), dtype=jnp.float32) * 0.1
        V = jax.random.normal(ks[4], (H, 2, D, 1), dtype=jnp.float32) * 0.1
        return {'X': X, 'local_pattern': local, 'long_range_pattern': longr, 'W': W, 'V': V, 'enc_bn_gamma': jnp.ones((F,), jnp.float32), 'enc_bn_beta': jnp.zeros((F,), jnp.float32), 'enc_mlp_W': jax.random.normal(ks[5], (F, F), dtype=jnp.float32) * 0.02, 'enc_mlp_b': jnp.zeros((F,), jnp.float32), 'enc_mlp_bn_gamma': jnp.ones((F,), jnp.float32), 'enc_mlp_bn_beta': jnp.zeros((F,), jnp.float32), 'dec_mlp_W': jax.random.normal(ks[6], (F, F), dtype=jnp.float32) * 0.02, 'dec_mlp_b': jnp.zeros((F,), jnp.float32), 'dec_mlp_bn_gamma': jnp.ones((F,), jnp.float32), 'dec_mlp_bn_beta': jnp.zeros((F,), jnp.float32)}
    _L1_gnn_all = _L1_gnn_setup()
    _L1_gnn_in = {k: v for k, v in _L1_gnn_all.items() if k in ('W', 'V', 'enc_bn_gamma', 'enc_bn_beta', 'enc_mlp_W', 'enc_mlp_b', 'enc_mlp_bn_gamma', 'enc_mlp_bn_beta', 'dec_mlp_W', 'dec_mlp_b', 'dec_mlp_bn_gamma', 'dec_mlp_bn_beta')}
    del _L1_gnn_all
    return {'x': x, 'adj': adj, 'L0_gnn_Wq': _L0_gnn_in['Wq'], 'L0_gnn_bq': _L0_gnn_in['bq'], 'L0_gnn_Wk': _L0_gnn_in['Wk'], 'L0_gnn_bk': _L0_gnn_in['bk'], 'L0_gnn_Wv': _L0_gnn_in['Wv'], 'L0_gnn_bv': _L0_gnn_in['bv'], 'L1_gnn_W': _L1_gnn_in['W'], 'L1_gnn_V': _L1_gnn_in['V'], 'L1_gnn_enc_bn_gamma': _L1_gnn_in['enc_bn_gamma'], 'L1_gnn_enc_bn_beta': _L1_gnn_in['enc_bn_beta'], 'L1_gnn_enc_mlp_W': _L1_gnn_in['enc_mlp_W'], 'L1_gnn_enc_mlp_b': _L1_gnn_in['enc_mlp_b'], 'L1_gnn_enc_mlp_bn_gamma': _L1_gnn_in['enc_mlp_bn_gamma'], 'L1_gnn_enc_mlp_bn_beta': _L1_gnn_in['enc_mlp_bn_beta'], 'L1_gnn_dec_mlp_W': _L1_gnn_in['dec_mlp_W'], 'L1_gnn_dec_mlp_b': _L1_gnn_in['dec_mlp_b'], 'L1_gnn_dec_mlp_bn_gamma': _L1_gnn_in['dec_mlp_bn_gamma'], 'L1_gnn_dec_mlp_bn_beta': _L1_gnn_in['dec_mlp_bn_beta']}

def reference(x, adj, L0_gnn_Wq, L0_gnn_bq, L0_gnn_Wk, L0_gnn_bk, L0_gnn_Wv, L0_gnn_bv, L1_gnn_W, L1_gnn_V, L1_gnn_enc_bn_gamma, L1_gnn_enc_bn_beta, L1_gnn_enc_mlp_W, L1_gnn_enc_mlp_b, L1_gnn_enc_mlp_bn_gamma, L1_gnn_enc_mlp_bn_beta, L1_gnn_dec_mlp_W, L1_gnn_dec_mlp_b, L1_gnn_dec_mlp_bn_gamma, L1_gnn_dec_mlp_bn_beta):
    import jax
    import jax.numpy as jnp

    def _L0_gnn_ref(x, spatial_encoding, edge_encoding, Wq, bq, Wk, bk, Wv, bv):
        import jax, jax.numpy as jnp
        import numpy as np
        N = 4096
        D = 256
        q = x @ Wq.T + bq
        k = x @ Wk.T + bk
        v = x @ Wv.T + bv
        scale = 1.0 / jnp.sqrt(jnp.asarray(q.shape[-1], q.dtype))
        a = q @ k.T * scale + spatial_encoding + edge_encoding
        attn = jax.nn.softmax(a, axis=-1)
        return attn @ v

    def _L1_gnn_ref(X, local_pattern, long_range_pattern, W, V, enc_bn_gamma, enc_bn_beta, enc_mlp_W, enc_mlp_b, enc_mlp_bn_gamma, enc_mlp_bn_beta, dec_mlp_W, dec_mlp_b, dec_mlp_bn_gamma, dec_mlp_bn_beta):
        import jax, jax.numpy as jnp
        import numpy as np
        N, F, H = (1536, 256, 4)
        D = F // H
        ALPHA = 0.5
        EPS = 1e-06

        def _batchnorm(x, gamma, beta):
            m = jnp.mean(x, axis=0)
            v = jnp.var(x, axis=0)
            return (x - m) * jax.lax.rsqrt(v + EPS) * gamma + beta

        def _masked_softmax(scores, mask):
            s = jnp.where(mask, scores, -jnp.inf)
            att = jax.nn.softmax(s, axis=-1)
            return jnp.where(mask, att, 0.0)

        def _mlp_block(x, Wm, bm, g, b):
            h = jax.nn.elu(x @ Wm.T + bm) + x
            return _batchnorm(h, g, b)
        n = X.shape[0]
        Xh = X.reshape(n, H, D).transpose(1, 0, 2)
        Xw = jnp.einsum('hnd,hde->hne', Xh, W)
        f1 = jnp.einsum('hnd,hd->hn', Xw, V[:, 0, :, 0])
        f2 = jnp.einsum('hnd,hd->hn', Xw, V[:, 1, :, 0])
        sig = jax.nn.sigmoid(f1[:, :, None] + f2[:, None, :])
        lmask = (local_pattern != 0)[None]
        gmask = (long_range_pattern != 0)[None]
        local_att = _masked_softmax(local_pattern[None] * sig, lmask)
        long_att = _masked_softmax(long_range_pattern[None] * sig, gmask)
        att = ALPHA * long_att + (1.0 - ALPHA) * local_att
        Xa = jnp.einsum('hij,hjd->hid', att, Xw)
        Xc = Xa.transpose(1, 0, 2).reshape(n, F)
        Xn = _batchnorm(Xc, enc_bn_gamma, enc_bn_beta)
        emb = _mlp_block(Xn, enc_mlp_W, enc_mlp_b, enc_mlp_bn_gamma, enc_mlp_bn_beta)
        Yh = emb.reshape(n, H, D).transpose(1, 0, 2)
        Y = jnp.einsum('hij,hjd->hid', att, Yh)
        Y = jnp.einsum('hnd,hed->hne', Y, W)
        Yc = Y.transpose(1, 0, 2).reshape(n, F)
        Yc = jax.nn.elu(Yc)
        out = _mlp_block(Yc, dec_mlp_W, dec_mlp_b, dec_mlp_bn_gamma, dec_mlp_bn_beta)
        return out
    h = jnp.maximum(_layernorm(x, axis=-1), 0.0)
    x = x + _L0_gnn_ref(h, adj, adj, L0_gnn_Wq, L0_gnn_bq, L0_gnn_Wk, L0_gnn_bk, L0_gnn_Wv, L0_gnn_bv)
    h = jnp.maximum(_layernorm(x, axis=-1), 0.0)
    x = x + _L1_gnn_ref(h, adj, adj, L1_gnn_W, L1_gnn_V, L1_gnn_enc_bn_gamma, L1_gnn_enc_bn_beta, L1_gnn_enc_mlp_W, L1_gnn_enc_mlp_b, L1_gnn_enc_mlp_bn_gamma, L1_gnn_enc_mlp_bn_beta, L1_gnn_dec_mlp_W, L1_gnn_dec_mlp_b, L1_gnn_dec_mlp_bn_gamma, L1_gnn_dec_mlp_bn_beta)
    return x

_drawn_inputs = setup_inputs


def setup_inputs(seed=0):
    import zlib

    import numpy as np

    out = dict(_drawn_inputs(seed))
    spreads = {'L0_gnn_bq': (0.0, 0.644),
     'L0_gnn_bk': (0.0, 0.8),
     'L0_gnn_bv': (0.0, 0.1),
     'L1_gnn_enc_bn_gamma': (1.0, 0.2),
     'L1_gnn_enc_bn_beta': (0.0, 0.8),
     'L1_gnn_enc_mlp_b': (0.0, 0.8),
     'L1_gnn_enc_mlp_bn_gamma': (1.0, 0.2),
     'L1_gnn_enc_mlp_bn_beta': (0.0, 0.55),
     'L1_gnn_dec_mlp_b': (0.0, 0.8),
     'L1_gnn_dec_mlp_bn_gamma': (1.0, 0.2),
     'L1_gnn_dec_mlp_bn_beta': (0.0, 0.1)}
    factors = {}
    for name, (base, spread) in spreads.items():
        noise = np.random.default_rng([zlib.crc32(name.encode()), seed]).standard_normal(out[name].shape)
        drawn = base * np.exp(spread * noise) if base else spread * noise
        out[name] = jnp.asarray(drawn.astype(out[name].dtype))
    for name, factor in factors.items():
        out[name] = (out[name] * factor).astype(out[name].dtype)
    return out
```

```python
from contextlib import ExitStack

import concourse.bass as bass
from concourse import mybir

ALU = mybir.AluOpType
ACT = mybir.ActivationFunctionType
AX_X = mybir.AxisListType.X
F32 = mybir.dt.float32
F32R = mybir.dt.float32r

P = 128
KIB = 1024
BIG = 1.0e36
ROW_FLOOR = -1.0e27
ABOVE_ONE = 1.0 + 2.0 ** -23
LN_EPS = 1e-5
BN_EPS = 1e-6

BQ, BK, ENC_G, ENC_B, EMLP_B, EMLP_G, EMLP_BETA, DMLP_B, DMLP_G, DMLP_BETA = range(10)


def build(nc, x, adj, wqT, wkT, wvT, bv, cols, w_head, w_headT, v_head, enc_wT, dec_wT, out):
    N, D = x.shape
    H, E, _ = w_head.shape
    T = N // P
    KC = D // P
    CH = 512
    NCH = N // CH
    TPC = CH // P
    assert E * H == D and KC == 2 and H == 4 and T == 16

    adjm_dram = nc.dram_tensor("adjm_dram", [N, N], F32)
    att_dram = nc.dram_tensor("att_dram", [T * H, P, N], F32)

    with ExitStack() as ctx:
        def small(name, shape, dt=F32):
            return ctx.enter_context(nc.sbuf_tensor(name, shape, dt))

        def sem(name):
            return ctx.enter_context(nc.semaphore(name))

        ident = small("ident", [P, P])
        vec = small("vec", [P, 10, KC])
        bq_s = small("bq_s", [P, KC])
        neg_half = small("neg_half", [P, T])
        wx = small("wx", [P, KC, P + 4])
        wTbd = small("wTbd", [P, KC, P])
        vbd = small("vbd", [P, KC, 4])
        fnat = small("fnat", [P, T, 2 * H])
        stats1 = small("stats1", [P, 6])
        mv1 = small("mv1", [P, T, 2])
        veps = small("veps", [P, T])
        rstd1 = small("rstd1", [P, T])
        cmax = small("cmax", [P, 2, NCH])
        rmax = small("rmax", [P, 2])
        negm = small("negm", [P, 2])
        rsum = small("rsum", [P, 2])
        rinv = small("rinv", [P, 1])
        mv2 = small("mv2", [P, 2])
        veps2 = small("veps2", [P, 1])
        rstd2 = small("rstd2", [P, 1])
        fcur = small("fcur", [P, 2, H])
        hmax = small("hmax", [P, 2, H])
        hneg = small("hneg", [P, 2, H])
        hsum = small("hsum", [P, 2, H])
        hval = small("hval", [P, H])
        hrec = small("hrec", [P, H])
        hinv = small("hinv", [P, H, E])
        bnst = small("bnst", [P, KC, T, 6])
        bnmv = small("bnmv", [P, KC, 2])
        bnve = small("bnve", [P, KC])
        bnrs = small("bnrs", [P, KC])
        bna = small("bna", [P, KC])
        bnt = small("bnt", [P, KC])
        bnb = small("bnb", [P, KC])
        xt = small("xt", [P, D])
        hn = small("hn", [P, D])
        h2T = small("h2T", [P, KC, P])

        base = 16 * KIB
        def at(name, shape, kib, dt=F32):
            return nc.alloc_sbuf_tensor_at(name, shape, dt, offset=base + kib * KIB)

        x_sb = at("x_sb", [P, T, D], 0)
        xw = at("xw", [P, T, D], 16)
        hn_all = at("hn_all", [P, T, D], 16)
        emb = at("emb", [P, T, D], 16)
        qhl = at("qhl", [P, 2 * KC, N], 32, F32R)
        khl = at("khl", [P, 2 * KC, N], 64, F32R)
        vhl = at("vhl", [P, T, 2 * D], 96, F32R)
        f2b = at("f2b", [P, H, N], 32)
        eb = at("eb", [P, H, N], 64)
        att = at("att", [P, H, N], 96)
        ring = [at("ringA", [P, H, N], 96), at("ringB", [P, H, N], 64), at("ringC", [P, H, N], 32)]
        adjt = at("adjt", [P, 2, N], 128)
        sc = at("sc", [P, 2, N], 144)
        hT = at("hT", [P, KC, N], 144)
        xc = at("xc", [P, KC, N], 144)
        hd = at("hd", [P, KC, N], 144)
        msk = at("msk", [P, 2, N], 160)
        tmpa = at("tmpa", [P, 4, CH], 160)
        hb = at("hb", [P, KC, N], 160)
        att_hl = at("att_hl", [P, 2, N], 176, F32R)
        wqkv = at("wqkv", [P, 3, KC, D], 176)
        bvb = at("bvb", [P, D], 182)
        rb = at("rb", [P, KC, N], 176)
        et = at("et", [P, 8, CH], 128)
        yt = at("yt", [P, KC, P], 128)
        yc = at("yc", [P, KC, P], 129)
        e1 = at("e1", [P, KC, P], 130)
        t1 = at("t1", [P, KC, P], 131)
        e2 = at("e2", [P, KC, P], 132)
        r2 = at("r2", [P, KC, P], 133)
        t2 = at("t2", [P, KC, P], 134)
        qcur = at("qcur", [P, 2, 2 * KC, P], -4, F32R)
        wmlp = at("wmlp", [P, 2, KC, D], -4)
        ob = at("ob", [P, T, D], 64)

        banks = [ctx.enter_context(nc.psum_tensor(f"banks{b}", [P, 2, CH], F32)) for b in range(4)]
        bank = [banks[b // 2][:, b % 2] for b in range(8)]

        weights_in = sem("weights_in")
        x_in = sem("x_in")
        adj_in = [sem(f"adj_in{b}") for b in range(2)]
        wmlp_in = sem("wmlp_in")
        const_ready = sem("const_ready")
        bq_ready = sem("bq_ready")
        zeroed = sem("zeroed")
        wv_done = sem("wv_done")
        wx_ready = sem("wx_ready")
        ln1_stats = sem("ln1_stats")
        ln1_mv = sem("ln1_mv")
        ln1_veps = sem("ln1_veps")
        ln1_rstd = sem("ln1_rstd")
        hn_all_ready = sem("hn_all_ready")
        hT_filled = sem("hT_filled")
        hT_ready = sem("hT_ready")
        qk_done = sem("qk_done")
        qk_copied = sem("qk_copied")
        qk_headed = sem("qk_headed")
        qk_split = sem("qk_split")
        v_done = sem("v_done")
        v_copied = sem("v_copied")
        v_headed = sem("v_headed")
        v_split = sem("v_split")

        qcur_ready = sem("qcur_ready")
        scores_ready = sem("scores_ready")
        scores_used = sem("scores_used")
        rmax_ready = sem("rmax_ready")
        negm_ready = sem("negm_ready")
        probs_ready = sem("probs_ready")
        probsT_filled = sem("probsT_filled")
        probsT_head = sem("probsT_head")
        probsT_rest = sem("probsT_rest")
        pv_group = sem("pv_group")
        mask_ready = sem("mask_ready")
        masked = sem("masked")
        adjm_out = [sem(f"adjm_out{b}") for b in range(2)]
        rinv_ready = sem("rinv_ready")
        xt_ready = sem("xt_ready")
        x1_ready = sem("x1_ready")
        ln2_stats = sem("ln2_stats")
        ln2_mv = sem("ln2_mv")
        ln2_veps = sem("ln2_veps")
        ln2_rstd = sem("ln2_rstd")
        hn_ready = sem("hn_ready")
        hnT_filled = sem("hnT_filled")
        h2T_ready = sem("h2T_ready")
        xw_done = sem("xw_done")
        xw_copied = sem("xw_copied")

        f2_filled = sem("f2_filled")
        f2_act = sem("f2_act")
        f2_dve = sem("f2_dve")

        adjm_in = [sem(f"adjm_in{b}") for b in range(2)]
        fcur_ready = sem("fcur_ready")
        tanh_ready = sem("tanh_ready")
        sig_ready = sem("sig_ready")
        hmax_ready = sem("hmax_ready")
        hneg_ready = sem("hneg_ready")
        exp_ready = sem("exp_ready")
        eT_filled = sem("eT_filled")
        attA = sem("attA")
        attB = sem("attB")
        pair_done = sem("pair_done")
        att_out = [sem(f"att_out{h}") for h in range(H)]
        hval_ready = sem("hval_ready")
        hrec_ready = sem("hrec_ready")
        hinv_ready = sem("hinv_ready")
        rbT_filled = sem("rbT_filled")
        rb_ready = sem("rb_ready")
        xc_ready = sem("xc_ready")
        xc_stats = sem("xc_stats")

        bn_mv = sem("bn_mv")
        bn_ve = sem("bn_ve")
        bn_rs = sem("bn_rs")
        bn_a = sem("bn_a")
        bn_t = sem("bn_t")
        bn_b = sem("bn_b")
        xn0_ready = sem("xn0_ready")
        xn1_ready = sem("xn1_ready")
        z_done = sem("z_done")
        z_exp = sem("z_exp")
        z_relu = sem("z_relu")
        z_t = sem("z_t")
        hb_ready = sem("hb_ready")
        hb_stats = sem("hb_stats")
        hbn0_ready = sem("hbn0_ready")
        hbn1_ready = sem("hbn1_ready")
        embT_filled = sem("embT_filled")
        emb_act = sem("emb_act")
        emb_dve = sem("emb_dve")

        ring_in = [sem(f"ring_in{b}") for b in range(3)]
        y_done = sem("y_done")
        yt_ready = sem("yt_ready")
        yw_done = sem("yw_done")
        e1_ready = sem("e1_ready")
        t1_ready = sem("t1_ready")
        yc_ready = sem("yc_ready")
        zd_done = sem("zd_done")
        zd_exp = sem("zd_exp")
        t2_ready = sem("t2_ready")
        hd_ready = sem("hd_ready")
        hd_stats = sem("hd_stats")
        hdn0_ready = sem("hdn0_ready")
        hdn1_ready = sem("hdn1_ready")
        oT_filled = sem("oT_filled")
        o_ready = sem("o_ready")
        out_stored = sem("out_stored")
        waits_apart = [sem(f"waits_apart{n}") for n in range(2)]

        block = ctx.enter_context(nc.Block())

        def wait(eng, s, value):
            if not isinstance(value, int) or value > 0:
                eng.wait_ge(s, value)

        def wait_apart(eng, s, value):
            if isinstance(value, int):
                wait(eng, s, value)
            else:
                eng.wait_ge(s, value).then_inc(waits_apart[eng is nc.vector], 1)

        def tile_no(i, count=T):
            if isinstance(i, int):
                return i
            return nc.s_assert_within(i, 0, count - 1, skip_runtime_bounds_check_because="the loop's count is fixed")

        def tile_cols(i):
            return bass.ds(tile_no(i) * P, P)

        def tile_row(i):
            return bass.ds(tile_no(i), 1)

        def loads(i, b):
            return 8 * i + (8 if b else 16)

        N_QK = 2 * KC * NCH
        N_WEIGHT_DMAS = 3 + 1 + 1 + 3 * H

        @block.sync
        def _(sp):
            sp.dma_start(x_sb[:], x.rearrange("(t p) d -> p t d", p=P)).then_inc(x_in, 16)
            for n, w in enumerate((wqT, wkT, wvT)):
                sp.dma_start(wqkv[:, n], w.rearrange("(c p) d -> p c d", p=P)).then_inc(weights_in, 16)
            sp.dma_start(vec[:], cols).then_inc(weights_in, 16)
            sp.dma_start(bvb[:], bv.partition_broadcast(P)).then_inc(weights_in, 16)
            sp.wait_ge(zeroed, 3)
            for h in range(H):
                c, r = h // 2, E * (h % 2)
                sp.dma_start(wx[r:r + E, c, r:r + E], w_head[h]).then_inc(weights_in, 16)
                sp.dma_start(wTbd[r:r + E, c, r:r + E], w_headT[h]).then_inc(weights_in, 16)
                sp.dma_start(vbd[r:r + E, c, 2 * (h % 2):2 * (h % 2) + 2], v_head[h]).then_inc(weights_in, 16)
            for k in range(2):
                sp.dma_start(adjt[:, k], adj[k * P:(k + 1) * P, :]).then_inc(adj_in[k], 16)

            def rows(k, b, more):
                sp.wait_ge(masked, k + 1)
                sp.dma_start(adjm_dram[tile_cols(k), :], msk[:, b]).then_inc(adjm_out[b], 16)
                if more:
                    sp.dma_start(adjt[:, b], adj[tile_cols(k + 2), :]).then_inc(adj_in[b], 16)

            with sp.Fori(0, T - 2, 2) as k:
                for b in range(2):
                    rows(k + b, b, True)
            for b in range(2):
                rows(T - 2 + b, b, False)

            sp.wait_ge(scores_ready, NCH * T)
            for n, w in enumerate((enc_wT, dec_wT)):
                sp.dma_start(wmlp[:, n], w.rearrange("(c p) d -> p c d", p=P)).then_inc(wmlp_in, 16)

            for b in range(2):
                sp.wait_ge(adjm_out[b], 16 * (T // 2))
            sp.dma_start(adjt[:, 0], adjm_dram[0:P, :]).then_inc(adjm_in[0], 16)

            def load_adjm(i, b):
                wait(sp, hmax_ready, H * (i - 1))
                sp.dma_start(adjt[:, b], adjm_dram[tile_cols(i), :]).then_inc(adjm_in[b], 16)

            def store_att(u, h):
                sp.wait_ge(attB, 2 * (u + 1))
                sp.wait_ge(attA, u + 1)
                sp.dma_start(att_dram[bass.ds(tile_no(u, T * H), 1)].rearrange("o p n -> p (o n)"),
                             att[:, h]).then_inc(att_out[h], 16)

            def spill(i, b, first=False, last=False):
                for h in range(H):
                    if h == 0 and not last:
                        load_adjm(i + 1, 1 - b)
                    if h == 0 and not first:
                        store_att(H * i - 1, H - 1)
                    if h > 0 and not last:
                        store_att(H * i + h - 1, h - 1)

            spill(0, 0, first=True)
            with sp.Fori(1, T - 1, 2) as i:
                spill(i, 1)
                spill(i + 1, 0)
            spill(T - 1, 1, last=True)

            def load_ring(b, tile):
                sp.dma_start(ring[b][:], att_dram[bass.ds(H * tile_no(tile), H)].rearrange("h p n -> p h n")
                             ).then_inc(ring_in[b], 16)
            for h in range(H):
                sp.wait_ge(att_out[h], 16 * (T - 1))
            sp.wait_ge(eT_filled, 3 * H * T)
            load_ring(1, 0)
            sp.wait_ge(tanh_ready, H * T)
            load_ring(2, 1)
            sp.wait_ge(y_done, KC)
            load_ring(0, 2)
            with sp.Fori(1, (T - 1) // 3) as r:
                for b in range(3):
                    n, buf = 3 * r + b + 1, (b + 1) % 3
                    sp.wait_ge(y_done, KC * (n - 2))
                    load_ring(buf, n - 1)

            for c in range(NCH):
                sp.wait_ge(o_ready, 2 * (c + 1))
                sp.dma_start(out[c * CH:(c + 1) * CH, :].rearrange("(t p) d -> p t d", p=P),
                             ob[:, TPC * c:TPC * (c + 1)]).then_inc(out_stored, 16)
            sp.wait_ge(out_stored, 16 * NCH)

        @block.gpsimd
        def _(pool):
            pool.memset(wx[:], 0.0).then_inc(zeroed, 1)
            pool.memset(wTbd[:], 0.0).then_inc(zeroed, 1)
            pool.memset(vbd[:], 0.0).then_inc(zeroed, 1)
            pool.memset(neg_half[:], -0.5).then_inc(const_ready, 1)
            pool.memset(ident[:], 0.0).then_inc(const_ready, 1)
            pool.wait_ge(const_ready, 2)
            pool.affine_select(out=ident[:], in_=ident[:], compare_op=ALU.not_equal, fill=1.0,
                               base=0, pattern=[[-1, P]], channel_multiplier=1).then_inc(const_ready, 1)
            pool.wait_ge(ln1_veps, 1)
            pool.tensor_tensor(rstd1[:], veps[:], neg_half[:], ALU.pow).then_inc(ln1_rstd, 1)

            def copy_q(k, b):
                pool.tensor_copy(qcur[:, b], qhl[:, :, tile_cols(k)]).then_inc(qcur_ready, 1)

            pool.wait_ge(qk_split, N_QK)
            copy_q(0, 0)
            copy_q(1, 1)

            def rstd_row():
                pool.tensor_tensor(rstd2[:], veps2[:], neg_half[:, 0:1], ALU.pow).then_inc(ln2_rstd, 1)

            for k in range(2):
                pool.wait_ge(scores_ready, NCH * (k + 1))
                copy_q(k + 2, k)
            with pool.Fori(2, T - 2, 2) as k:
                for b in range(2):
                    pool.wait_ge(ln2_veps, k + b - 1)
                    rstd_row()
                    pool.wait_ge(scores_ready, NCH * (k + b + 1))
                    copy_q(k + b + 2, b)
            for k in range(T - 2, T + 2):
                pool.wait_ge(ln2_veps, k - 1)
                rstd_row()
            def spread_inverse(i):
                pool.wait_ge(hval_ready, i + 1)
                wait(pool, rbT_filled, KC * i)
                pool.wait_ge(hrec_ready, i + 1)
                pool.tensor_tensor(hinv[:], hval[:].unsqueeze(2).broadcast_to([P, H, E]),
                                   hrec[:].unsqueeze(2).broadcast_to([P, H, E]), ALU.mult
                                   ).then_inc(hinv_ready, 1)

            def sigmoid(i, h):
                wait_apart(pool, tanh_ready, H * i + h + 1)
                pool.tensor_scalar(eb[:, h], eb[:, h], ABOVE_ONE, 0.5, ALU.add, ALU.mult).then_inc(sig_ready, 1)

            for h in range(H):
                sigmoid(0, h)
            with pool.Fori(1, T) as i:
                for h in range(H):
                    sigmoid(i, h)
                    if h == 2:
                        spread_inverse(i - 1)
            spread_inverse(T - 1)
            for n in range(3):
                pool.wait_ge(bn_ve, n + 1)
                pool.tensor_tensor(bnrs[:], bnve[:], neg_half[:, 0:KC], ALU.pow).then_inc(bn_rs, 1)

        @block.scalar
        def _(act):
            act.wait_ge(weights_in, 16 * N_WEIGHT_DMAS)
            act.activation(bq_s[:], vec[:, BQ], ACT.Copy, scale=1.0 / 32).then_inc(bq_ready, 1)
            act.wait_ge(bq_ready, 1)
            nqk = 0
            for g in range(NCH):
                for c in range(KC):
                    act.wait_ge(hT_filled, KC * g + c + 1)
                    act.activation(hT[:, c, g * CH:(g + 1) * CH], bank[4 + c][:], ACT.Relu
                                   ).then_inc(hT_ready, 1)
                for which in range(2):
                    for c in range(KC):
                        act.wait_ge(qk_done, nqk + 1)
                        wait(act, qk_split, nqk - 3)
                        bias = bq_s[:, c:c + 1] if which == 0 else vec[:, BK, c:c + 1]
                        act.activation(tmpa[:, nqk % 4], bank[nqk % 4][:], ACT.Identity, bias=bias,
                                       scale=1.0 / 32 if which == 0 else 1.0).then_inc(qk_copied, 1)
                        nqk += 1

            def probs(k, b):
                act.wait_ge(negm_ready, k + 1)
                act.activation(sc[:, b], sc[:, b], ACT.Exp, bias=negm[:, b:b + 1],
                               accum_out=rsum[:, b:b + 1]).then_inc(probs_ready, 1)

            def head(k, g):
                act.wait_ge(probsT_filled, NCH * k + g + 1)
                wait(act, pv_group, NCH * (k - 1) + g + 1)
                act.activation(att_hl[:, 0, g * CH:(g + 1) * CH], bank[4 + g % 2][:], ACT.Copy
                               ).then_inc(probsT_head, 1)

            def relu_hnT(k):
                act.wait_ge(hnT_filled, k + 1)
                act.activation(h2T[:], bank[7][:, 0:D].rearrange("p (c n) -> p c n", c=KC), ACT.Relu
                               ).then_inc(h2T_ready, 1)

            def copy_xw(k):
                act.wait_ge(xw_done, k + 1)
                both = bank[7][:, 0:KC * (P + 4)].rearrange("p (c n) -> p c n", c=KC)
                act.activation(xw[:, tile_row(k)].rearrange("p o (c n) -> p (o c) n", c=KC),
                               both[:, :, 0:P], ACT.Copy).then_inc(xw_copied, 1)
                act.activation(fnat[:, tile_row(k)].rearrange("p o (c n) -> p (o c) n", c=KC),
                               both[:, :, P:P + 4], ACT.Copy).then_inc(xw_copied, 1)

            def tile_b(k, b, scores=True, transposed=True, norm=True):
                if norm:
                    relu_hnT(k - 2)
                if transposed:
                    for g in range(NCH):
                        head(k - 1, g)
                if scores:
                    probs(k, b)
                if norm:
                    copy_xw(k - 2)

            tile_b(0, 0, transposed=False, norm=False)
            tile_b(1, 1, norm=False)
            with act.Fori(2, T, 2) as k:
                tile_b(k, 0)
                tile_b(k + 1, 1)
            tile_b(T, 0, scores=False)
            tile_b(T + 1, 1, scores=False, transposed=False)

            for n in range(0, H * NCH, 2):
                act.wait_ge(f2_filled, n + 1)
                act.activation(f2b[:, n // NCH, (n % NCH) * CH:(n % NCH + 1) * CH], bank[n % 4][:],
                               ACT.Copy).then_inc(f2_act, 1)

            def tanh(i, b, h):
                if h == 0:
                    act.wait_ge(fcur_ready, i + 1)
                wait(act, eT_filled, 3 * (H * (i - 1) + h + 1))
                act.activation(eb[:, h], f2b[:, h], ACT.Tanh, bias=fcur[:, b, h:h + 1], scale=0.5
                               ).then_inc(tanh_ready, 1)

            def exp(i, b, h):
                act.wait_ge(hneg_ready, H * i + h + 1)
                act.activation(eb[:, h], eb[:, h], ACT.Exp, bias=hneg[:, b, h:h + 1],
                               accum_out=hsum[:, b, h:h + 1]).then_inc(exp_ready, 1)

            def copy_eT(i, h):
                act.wait_ge(eT_filled, 3 * (H * i + h) + 1)
                wait(act, pair_done, KC * (i - 1) + h // 2 + 1)
                wait(act, att_out[h], 16 * i)
                act.activation(att[:, h, 0:CH], bank[0][:], ACT.Copy).then_inc(attA, 1)

            def copy_rb(i, b):
                for c in range(KC):
                    act.wait_ge(rbT_filled, KC * i + c + 1)
                    act.activation(rb[:, c, tile_cols(i)], bank[4 + KC * b + c][:, P:2 * P], ACT.Copy
                                   ).then_inc(rb_ready, 1)

            def tile_d(i, b, first=False, last=False):
                for h in range(H):
                    if h < 2:
                        tanh(i, b, h + 2)
                    elif not last:
                        tanh(i + 1, 1 - b, h - 2)
                    if h > 0:
                        copy_eT(i, h - 1)
                    elif not first:
                        copy_eT(i - 1, H - 1)
                    exp(i, b, h)
                if not first:
                    copy_rb(i - 1, 1 - b)

            act.wait_ge(f2_act, H * NCH // 2)
            act.wait_ge(f2_dve, H * NCH // 2)
            tanh(0, 0, 0)
            tanh(0, 0, 1)
            tile_d(0, 0, first=True)
            tile_d(1, 1)
            tile_d(2, 0)
            with act.Fori(3, T - 1, 2) as i:
                tile_d(i, 1)
                tile_d(i + 1, 0)
            tile_d(T - 1, 1, last=True)
            copy_eT(T - 1, H - 1)
            copy_rb(T - 1, 1)

            act.wait_ge(bn_b, 1)
            for c in range(NCH):
                act.activation(xc[:, 1, c * CH:(c + 1) * CH], xc[:, 1, c * CH:(c + 1) * CH], ACT.Identity,
                               bias=bnb[:, 1:2], scale=bna[:, 1:2]).then_inc(xn1_ready, 1)
            for n in range(KC * NCH):
                f = n % KC
                act.wait_ge(z_done, n + 1)
                wait(act, hb_ready, n - 1)
                act.activation(et[:, n % 2], bank[n % 4][:], ACT.Exp, bias=vec[:, EMLP_B, f:f + 1]
                               ).then_inc(z_exp, 1)
                act.activation(et[:, 2 + n % 2], bank[n % 4][:], ACT.Relu, bias=vec[:, EMLP_B, f:f + 1]
                               ).then_inc(z_relu, 1)
            act.wait_ge(bn_b, 2)
            for c in range(NCH):
                act.activation(hb[:, 1, c * CH:(c + 1) * CH], hb[:, 1, c * CH:(c + 1) * CH], ACT.Identity,
                               bias=bnb[:, 1:2], scale=bna[:, 1:2]).then_inc(hbn1_ready, 1)
            for n in range(1, T // 2, 2):
                act.wait_ge(embT_filled, n + 1)
                act.activation(emb[:, 2 * n:2 * n + 2], bank[n % 4][:].rearrange("p (t d) -> p t d", t=2),
                               ACT.Copy).then_inc(emb_act, 1)

            def elu_in(n):
                act.wait_ge(yw_done, n + 1)
                act.activation(e1[:], bank[2][:, 0:D].rearrange("p (c n) -> p c n", c=KC), ACT.Exp
                               ).then_inc(e1_ready, 1)

            def mlp_out(n):
                act.wait_ge(zd_done, n + 1)
                for f in range(KC):
                    act.activation(e2[:, f], bank[3][:, f * P:(f + 1) * P], ACT.Exp,
                                   bias=vec[:, DMLP_B, f:f + 1])
                    last = act.activation(r2[:, f], bank[3][:, f * P:(f + 1) * P], ACT.Relu,
                                          bias=vec[:, DMLP_B, f:f + 1])
                last.then_inc(zd_exp, 1)

            def step_f(n):
                wait(act, t1_ready, n - 1)
                elu_in(n - 1)
                wait(act, hd_ready, n - 1)
                mlp_out(n - 1)

            step_f(1)
            with act.Fori(2, T + 1) as n:
                step_f(n)

            act.wait_ge(bn_b, 3)
            for c in range(NCH):
                act.activation(hd[:, 1, c * CH:(c + 1) * CH], hd[:, 1, c * CH:(c + 1) * CH], ACT.Identity,
                               bias=bnb[:, 1:2], scale=bna[:, 1:2]).then_inc(hdn1_ready, 1)

        @block.tensor
        def _(pe):
            pe.wait_ge(const_ready, 3)
            pe.wait_ge(weights_in, 16 * N_WEIGHT_DMAS)
            for c in range(KC):
                last = pe.matmul(bank[7][:, 4 * c:4 * c + 4], wTbd[:, c], vbd[:, c])
            last.then_inc(wv_done, 1)
            nqk = nv = 0

            def transpose_h(g):
                for c in range(KC):
                    wait(pe, hT_ready, KC * (g - 1) + c + 1)
                    pe.wait_ge(hn_all_ready, TPC * (g + 1))
                    for t in range(TPC):
                        last = pe.transpose(bank[4 + c][:, t * P:(t + 1) * P],
                                            hn_all[:, TPC * g + t, c * P:(c + 1) * P], ident[:])
                    last.then_inc(hT_filled, 1)

            transpose_h(0)
            for g in range(NCH):
                if g + 1 < NCH:
                    transpose_h(g + 1)
                pe.wait_ge(hT_ready, KC * (g + 1))
                for which in range(2):
                    for f in range(KC):
                        wait(pe, qk_copied, nqk - 3)
                        for c in range(KC):
                            last = pe.matmul(bank[nqk % 4][:], wqkv[:, which, c, f * P:(f + 1) * P],
                                             hT[:, c, g * CH:(g + 1) * CH], start=(c == 0), stop=(c == KC - 1))
                        last.then_inc(qk_done, 1)
                        nqk += 1
                for t in range(TPC):
                    if nv == 0:
                        pe.wait_ge(wx_ready, 1)
                    wait(pe, v_copied, nv - 1)
                    for c in range(KC):
                        last = pe.matmul(bank[6 + nv % 2][:, 0:D],
                                         hT[:, c, nv * P:(nv + 1) * P], wqkv[:, 2, c], start=(c == 0),
                                         stop=(c == KC - 1))
                    last.then_inc(v_done, 1)
                    nv += 1

            def scores(k, b):
                pe.wait_ge(qcur_ready, k + 1)
                for n in range(NCH):
                    wait(pe, scores_used, NCH * (k - 1) + n + 1)
                    for c in range(KC):
                        for a, z in ((0, 0), (0, KC), (KC, 0)):
                            last = pe.matmul(bank[n][:], qcur[:, b, a + c], khl[:, z + c, n * CH:(n + 1) * CH],
                                             start=(c == 0 and a == z), stop=(c == KC - 1 and a > 0))
                    last.then_inc(scores_ready, 1)

            def transpose_probs(k, b, g):
                if g == 0:
                    pe.wait_ge(probs_ready, k + 1)
                wait(pe, probsT_rest, NCH * k + g - 1)
                for t in range(TPC):
                    last = pe.transpose(bank[4 + g % 2][:, t * P:(t + 1) * P],
                                        sc[:, b, g * CH + t * P:g * CH + (t + 1) * P], ident[:])
                last.then_inc(probsT_filled, 1)

            def attend(k, g):
                pv = bank[6]
                if g == 0:
                    wait(pe, x1_ready, k)
                jobs = [(0, t) for t in range(TPC)] + [(1, t) for t in range(TPC)]
                if g == NCH - 1:
                    jobs = jobs[:TPC - 1] + jobs[TPC:] + [jobs[TPC - 1]]
                for n, (part, t) in enumerate(jobs):
                    if n == 0:
                        pe.wait_ge(probsT_head, NCH * k + g + 1)
                    if part == 1 and t == 0:
                        pe.wait_ge(probsT_rest, NCH * k + g + 1)
                    j = TPC * g + t
                    width = D if part else 2 * D
                    last = pe.matmul(pv[:, 0:width], att_hl[:, part, j * P:(j + 1) * P], vhl[:, j, 0:width],
                                     start=(g == 0 and n == 0), stop=(g == NCH - 1 and n == 2 * TPC - 1))
                last.then_inc(pv_group, 1)

            def transpose_hn(k):
                pe.wait_ge(hn_ready, k + 1)
                wait(pe, xw_copied, 2 * k)
                for c in range(KC):
                    last = pe.transpose(bank[7][:, c * P:(c + 1) * P], hn[:, c * P:(c + 1) * P], ident[:])
                last.then_inc(hnT_filled, 1)

            def project_w(k):
                pe.wait_ge(h2T_ready, k + 1)
                for c in range(KC):
                    last = pe.matmul(bank[7][:, c * (P + 4):(c + 1) * (P + 4)], h2T[:, c], wx[:, c])
                last.then_inc(xw_done, 1)

            def tile_b(k, b, scored=True, attended=True, norm=True):
                if scored:
                    scores(k, b)
                if norm:
                    transpose_hn(k - 2)
                if attended:
                    transpose_probs(k - 1, 1 - b, 0)
                    for g in range(NCH):
                        if g + 1 < NCH:
                            transpose_probs(k - 1, 1 - b, g + 1)
                        attend(k - 1, g)
                if norm:
                    project_w(k - 2)

            pe.wait_ge(qk_split, N_QK)
            pe.wait_ge(v_split, T)
            tile_b(0, 0, attended=False, norm=False)
            tile_b(1, 1, norm=False)
            tile_b(2, 0)
            tile_b(3, 1)
            with pe.Fori(4, T, 2) as k:
                tile_b(k, 0)
                tile_b(k + 1, 1)
            tile_b(T, 0, scored=False)
            tile_b(T + 1, 1, scored=False, attended=False)

            pe.wait_ge(xw_copied, 2 * T)
            for n in range(H * NCH):
                h = n // NCH
                if n >= 4:
                    pe.wait_ge((f2_act, f2_dve)[n % 2], (n - 4) // 2 + 1)
                for t in range(TPC):
                    tile = TPC * (n % NCH) + t
                    last = pe.transpose(bank[n % 4][:, t * P:(t + 1) * P],
                                        fnat[:, tile, 2 * h + 1:2 * h + 2].broadcast_to([P, P]), ident[:])
                last.then_inc(f2_filled, 1)

            def transpose_e(i, h):
                pe.wait_ge(exp_ready, H * i + h + 1)
                u = H * i + h
                for n in range(NCH):
                    if n == 0:
                        wait(pe, attA, u)
                    elif n == 1:
                        wait(pe, attB, 2 * u - 1)
                    elif n == 2:
                        wait(pe, attB, 2 * u)
                    for t in range(TPC):
                        j = TPC * n + t
                        last = pe.transpose(bank[n][:, t * P:(t + 1) * P], eb[:, h, j * P:(j + 1) * P], ident[:])
                    if n != 2:
                        last.then_inc(eT_filled, 1)

            def attend_pair(i, b, c, half):
                if half == 0:
                    u = H * i + 2 * c + 2
                    pe.wait_ge(attA, u)
                    pe.wait_ge(attB, 2 * u)
                    wait(pe, xc_ready, KC * (i - 2) + c + 1)
                for j in range(half * T // 2, (half + 1) * T // 2):
                    for m in range(2):
                        h = 2 * c + m
                        last = pe.matmul(bank[4 + KC * b + c][m * E:(m + 1) * E, 0:P],
                                         xw[:, j, h * E:(h + 1) * E], att[:, h, j * P:(j + 1) * P],
                                         start=(j == 0), stop=(j == T - 1))
                if half:
                    last.then_inc(pair_done, 1)

            def spread_rinv(i, b):
                pe.wait_ge(hinv_ready, i + 1)
                for c in range(KC):
                    pe.transpose(bank[4 + KC * b + c][:, P:2 * P],
                                 hinv[:, 2 * c:2 * c + 2].rearrange("p h e -> p (h e)"), ident[:]
                                 ).then_inc(rbT_filled, 1)

            def tile_d(i, b, first=False):
                if not first:
                    transpose_e(i - 1, 3)
                    attend_pair(i - 1, 1 - b, 0, 1)
                transpose_e(i, 0)
                if not first:
                    attend_pair(i - 1, 1 - b, 1, 0)
                transpose_e(i, 1)
                if not first:
                    attend_pair(i - 1, 1 - b, 1, 1)
                    spread_rinv(i - 1, 1 - b)
                transpose_e(i, 2)
                attend_pair(i, b, 0, 0)

            pe.wait_ge(f2_act, H * NCH // 2)
            pe.wait_ge(f2_dve, H * NCH // 2)
            tile_d(0, 0, first=True)
            tile_d(1, 1)
            tile_d(2, 0)
            with pe.Fori(3, T - 1, 2) as i:
                tile_d(i, 1)
                tile_d(i + 1, 0)
            tile_d(T - 1, 1)
            transpose_e(T - 1, 3)
            attend_pair(T - 1, 1, 0, 1)
            attend_pair(T - 1, 1, 1, 0)
            attend_pair(T - 1, 1, 1, 1)
            spread_rinv(T - 1, 1)

            pe.wait_ge(wmlp_in, 32)
            for n in range(KC * NCH):
                c, f = n // KC, n % KC
                pe.wait_ge(xn0_ready, c + 1)
                pe.wait_ge(xn1_ready, c + 1)
                wait(pe, z_relu, n - 3)
                for a in range(KC):
                    last = pe.matmul(bank[n % 4][:], wmlp[:, 0, a, f * P:(f + 1) * P],
                                     xc[:, a, c * CH:(c + 1) * CH], start=(a == 0), stop=(a == KC - 1))
                last.then_inc(z_done, 1)
            for n in range(T // 2):
                c = 2 * n // TPC
                pe.wait_ge(hbn0_ready, c + 1)
                pe.wait_ge(hbn1_ready, c + 1)
                if n >= 4:
                    pe.wait_ge((emb_dve, emb_act)[n % 2], (n - 4) // 2 + 1)
                for t in range(2):
                    for a in range(KC):
                        j = 2 * n + t
                        last = pe.transpose(bank[n % 4][:, t * D + a * P:t * D + (a + 1) * P],
                                            hb[:, a, j * P:(j + 1) * P], ident[:])
                last.then_inc(embT_filled, 1)

            def attend_emb(n, src, c):
                wait(pe, yt_ready, KC * (n - 1) + c + 1)
                for j in range(T):
                    for m in range(2):
                        h = 2 * c + m
                        last = pe.matmul(bank[c][m * E:(m + 1) * E, 0:P], emb[:, j, h * E:(h + 1) * E],
                                         src[:, h, j * P:(j + 1) * P], start=(j == 0), stop=(j == T - 1))
                last.then_inc(y_done, 1)

            def times_w(n):
                pe.wait_ge(yt_ready, KC * (n + 1))
                wait(pe, yc_ready, n)
                for c in range(KC):
                    last = pe.matmul(bank[2][:, c * P:(c + 1) * P], wTbd[:, c], yt[:, c])
                last.then_inc(yw_done, 1)

            def mlp(n):
                pe.wait_ge(yc_ready, n + 1)
                wait(pe, zd_exp, n)
                for f in range(KC):
                    for a in range(KC):
                        last = pe.matmul(bank[3][:, f * P:(f + 1) * P], wmlp[:, 1, a, f * P:(f + 1) * P],
                                         yc[:, a], start=(a == 0), stop=(a == KC - 1))
                last.then_inc(zd_done, 1)

            pe.wait_ge(emb_act, T // 4)
            pe.wait_ge(emb_dve, T // 4)
            attend_emb(0, att, 0)
            attend_emb(0, att, 1)

            def three_steps(r):
                for b in range(3):
                    n, buf = 3 * r + b + 1, (b + 1) % 3
                    pe.wait_ge(ring_in[buf], 16 * (r + 1))
                    attend_emb(n, ring[buf], 0)
                    times_w(n - 1)
                    attend_emb(n, ring[buf], 1)
                    mlp(n - 1)

            three_steps(0)
            with pe.Fori(1, (T - 1) // 3) as r:
                three_steps(r)
            times_w(T - 1)
            mlp(T - 1)

            for n in range(T // 2):
                c = 2 * n // TPC
                pe.wait_ge(hdn0_ready, c + 1)
                pe.wait_ge(hdn1_ready, c + 1)
                wait(pe, o_ready, n - 3)
                for t in range(2):
                    for a in range(KC):
                        j = 2 * n + t
                        last = pe.transpose(bank[4 + n % 4][:, t * D + a * P:t * D + (a + 1) * P],
                                            hd[:, a, j * P:(j + 1) * P], ident[:])
                last.then_inc(oT_filled, 1)

        @block.vector
        def _(dve):
            dve.wait_ge(x_in, 16)
            for t in range(T):
                dve.bn_stats(bnst[:, 0, t], x_sb[:, t]).then_inc(ln1_stats, 1)
            for t in range(T):
                dve.wait_ge(ln1_stats, t + 1)
                dve.bn_aggr(mv1[:, t], bnst[:, 0, t]).then_inc(ln1_mv, 1)
            dve.wait_ge(ln1_mv, T)
            dve.tensor_scalar(veps[:], mv1[:, :, 1], LN_EPS, None, ALU.add).then_inc(ln1_veps, 1)
            dve.wait_ge(ln1_rstd, 1)
            for t in range(T):
                dve.tensor_scalar(hn_all[:, t], x_sb[:, t], mv1[:, t, 0:1], rstd1[:, t:t + 1],
                                  ALU.subtract, ALU.mult).then_inc(hn_all_ready, 1)
            dve.wait_ge(weights_in, 16 * N_WEIGHT_DMAS)
            dve.wait_ge(wv_done, 1)
            dve.tensor_copy(wx[:, :, P:P + 4], bank[7][:, 0:4 * KC].rearrange("p (c k) -> p c k", c=KC)
                            ).then_inc(wx_ready, 1)
            nqk = nv = 0
            vtmp = (xt, hn)
            for g in range(NCH):
                for which in range(2):
                    dst = (qhl, khl)[which]
                    for f in range(KC):
                        cs = slice(g * CH, (g + 1) * CH)
                        dve.wait_ge(qk_copied, nqk + 1)
                        dve.tensor_copy(dst[:, f, cs], tmpa[:, nqk % 4]).then_inc(qk_headed, 1)
                        dve.wait_ge(qk_headed, nqk + 1)
                        dve.tensor_tensor(dst[:, KC + f, cs], tmpa[:, nqk % 4], dst[:, f, cs].bitcast(F32),
                                          ALU.subtract).then_inc(qk_split, 1)
                        nqk += 1
                for t in range(TPC):
                    dve.wait_ge(v_done, nv + 1)
                    dve.tensor_tensor(vtmp[nv % 2][:], bank[6 + nv % 2][:, 0:D], bvb[:], ALU.add
                                      ).then_inc(v_copied, 1)
                    dve.wait_ge(v_copied, nv + 1)
                    dve.tensor_copy(vhl[:, nv, 0:D], vtmp[nv % 2][:]).then_inc(v_headed, 1)
                    dve.wait_ge(v_headed, nv + 1)
                    dve.tensor_tensor(vhl[:, nv, D:2 * D], vtmp[nv % 2][:], vhl[:, nv, 0:D].bitcast(F32),
                                      ALU.subtract).then_inc(v_split, 1)
                    nv += 1

            def score_rows(k, b, n):
                wait_apart(dve, scores_ready, NCH * k + n + 1)
                if n == 0:
                    wait_apart(dve, adj_in[b], loads(k, b))
                    wait_apart(dve, probsT_filled, NCH * (k - 1))
                cs = slice(n * CH, (n + 1) * CH)
                dve.tensor_tensor_reduce(sc[:, b, cs], bank[n][:], adjt[:, b, cs], 2.0, -3.0e38, ALU.add,
                                         ALU.max, cmax[:, b, n:n + 1]).then_inc(scores_used, 1)

            def row_max(k, b):
                dve.wait_ge(scores_used, NCH * (k + 1))
                dve.tensor_reduce(rmax[:, b:b + 1], cmax[:, b], AX_X, ALU.max).then_inc(rmax_ready, 1)
                dve.wait_ge(rmax_ready, k + 1)
                dve.tensor_scalar(negm[:, b:b + 1], rmax[:, b:b + 1], -1.0, None, ALU.mult
                                  ).then_inc(negm_ready, 1)

            def rest(k, g):
                dve.wait_ge(probsT_head, NCH * k + g + 1)
                wait(dve, pv_group, NCH * (k - 1) + g + 1)
                cs = slice(g * CH, (g + 1) * CH)
                dve.tensor_tensor(att_hl[:, 1, cs], bank[4 + g % 2][:], att_hl[:, 0, cs].bitcast(F32),
                                  ALU.subtract).then_inc(probsT_rest, 1)

            def mask_zero(k, b):
                wait(dve, adjm_out[b], loads(k, b) - 16)
                dve.tensor_scalar(msk[:, b], adjt[:, b], 0.0, -BIG, ALU.is_equal, ALU.mult
                                  ).then_inc(mask_ready, 1)

            def mask_add(k, b):
                dve.wait_ge(mask_ready, k + 1)
                dve.tensor_tensor(msk[:, b], msk[:, b], adjt[:, b], ALU.add).then_inc(masked, 1)

            def residual(k, b):
                row = x_sb[:, tile_row(k)].rearrange("p o d -> p (o d)")
                dve.wait_ge(pv_group, NCH * (k + 1))
                dve.reciprocal(rinv[:], rsum[:, b:b + 1]).then_inc(rinv_ready, 1)
                dve.wait_ge(rinv_ready, k + 1)
                dve.scalar_tensor_tensor(xt[:], bank[6][:, 0:D], rinv[:], row, ALU.mult, ALU.add
                                         ).then_inc(xt_ready, 1)
                dve.wait_ge(xt_ready, k + 1)
                dve.scalar_tensor_tensor(row, bank[6][:, D:2 * D], rinv[:], xt[:], ALU.mult, ALU.add
                                         ).then_inc(x1_ready, 1)
                wait_apart(dve, x1_ready, k + 1)
                dve.bn_stats(stats1[:], row).then_inc(ln2_stats, 1)
                wait_apart(dve, ln2_stats, k + 1)
                dve.bn_aggr(mv2[:], stats1[:]).then_inc(ln2_mv, 1)
                dve.wait_ge(ln2_mv, k + 1)
                dve.tensor_scalar(veps2[:], mv2[:, 1:2], LN_EPS, None, ALU.add).then_inc(ln2_veps, 1)

            def normalise(k):
                dve.wait_ge(ln2_rstd, k + 1)
                wait(dve, hnT_filled, k)
                dve.tensor_scalar(hn[:], x_sb[:, tile_row(k)].rearrange("p o d -> p (o d)"), mv2[:, 0:1],
                                  rstd2[:], ALU.subtract, ALU.mult).then_inc(hn_ready, 1)

            def tile_b(k, b, scored=True, attended=True, norm=True):
                if norm:
                    residual(k - 2, b)
                if scored:
                    score_rows(k, b, 0)
                if norm:
                    normalise(k - 2)
                if scored:
                    for n in range(1, NCH):
                        score_rows(k, b, n)
                    row_max(k, b)
                if attended:
                    rest(k - 1, 0)
                    rest(k - 1, 1)
                if scored:
                    mask_zero(k, b)
                if attended:
                    rest(k - 1, 2)
                    rest(k - 1, 3)
                if scored:
                    mask_add(k, b)

            tile_b(0, 0, attended=False, norm=False)
            tile_b(1, 1, norm=False)
            tile_b(2, 0)
            tile_b(3, 1)
            with dve.Fori(4, T, 2) as k:
                tile_b(k, 0)
                tile_b(k + 1, 1)
            tile_b(T, 0, scored=False)
            tile_b(T + 1, 1, scored=False, attended=False)

            for n in range(1, H * NCH, 2):
                dve.wait_ge(f2_filled, n + 1)
                dve.tensor_copy(f2b[:, n // NCH, (n % NCH) * CH:(n % NCH + 1) * CH], bank[n % 4][:]
                                ).then_inc(f2_dve, 1)

            def bias(i, b):
                wait(dve, tanh_ready, H * (i - 1))
                f1 = fnat[:, tile_row(i)].rearrange("p o (h k) -> p (o h) k", k=2)[:, :, 0]
                dve.tensor_scalar(fcur[:, b], f1, 0.5, None, ALU.mult).then_inc(fcur_ready, 1)

            def head_max(i, b, h):
                if h == 0:
                    wait_apart(dve, adjm_in[b], loads(i, b))
                wait_apart(dve, sig_ready, H * i + h + 1)
                dve.tensor_tensor_reduce(eb[:, h], eb[:, h], adjt[:, b], 1.0, -3.0e38, ALU.mult, ALU.max,
                                         hmax[:, b, h:h + 1]).then_inc(hmax_ready, 1)
                dve.wait_ge(hmax_ready, H * i + h + 1)
                dve.tensor_scalar(hneg[:, b, h:h + 1], hmax[:, b, h:h + 1], -1.0, None, ALU.mult
                                  ).then_inc(hneg_ready, 1)

            def copy_eT(i, h):
                dve.wait_ge(eT_filled, 3 * (H * i + h) + 2)
                wait(dve, pair_done, KC * (i - 1) + h // 2 + 1)
                wait(dve, att_out[h], 16 * i)
                dve.tensor_copy(att[:, h, CH:2 * CH], bank[1][:]).then_inc(attB, 1)
                dve.wait_ge(eT_filled, 3 * (H * i + h) + 3)
                dve.tensor_copy(att[:, h, 2 * CH:4 * CH].rearrange("p (b n) -> p b n", b=2), banks[1][:]
                                ).then_inc(attB, 1)

            def row_inverse(i, b):
                dve.wait_ge(exp_ready, H * (i + 1))
                wait(dve, hinv_ready, i)
                dve.tensor_scalar(hval[:], hmax[:, b], ROW_FLOOR, None, ALU.is_gt).then_inc(hval_ready, 1)
                dve.reciprocal(hrec[:], hsum[:, b]).then_inc(hrec_ready, 1)

            def scale_xc(i, b):
                for c in range(KC):
                    dve.wait_ge(rb_ready, KC * i + c + 1)
                    dve.wait_ge(pair_done, KC * i + c + 1)
                    dve.tensor_tensor(xc[:, c, tile_cols(i)], bank[4 + KC * b + c][:, 0:P], rb[:, c, tile_cols(i)],
                                      ALU.mult).then_inc(xc_ready, 1)
                for c in range(KC):
                    wait_apart(dve, xc_ready, KC * i + c + 1)
                    dve.bn_stats(bnst[:, c, tile_row(i)].rearrange("p o s -> p (o s)"),
                                 xc[:, c, tile_cols(i)]).then_inc(xc_stats, 1)

            def tile_d(i, b, first=False, last=False):
                for h in range(H):
                    ahead = (i, b, h + 1) if h + 1 < H else (i + 1, 1 - b, 0)
                    more = h + 1 < H or not last
                    if h == 0 and not last:
                        bias(i + 1, 1 - b)
                    if more:
                        head_max(*ahead)
                    if h > 0:
                        copy_eT(i, h - 1)
                    elif not first:
                        copy_eT(i - 1, H - 1)
                        row_inverse(i - 1, 1 - b)
                if not first:
                    scale_xc(i - 1, 1 - b)

            dve.wait_ge(xw_copied, 2 * T)
            bias(0, 0)
            head_max(0, 0, 0)
            tile_d(0, 0, first=True)
            tile_d(1, 1)
            tile_d(2, 0)
            with dve.Fori(3, T - 1, 2) as i:
                tile_d(i, 1)
                tile_d(i + 1, 0)
            tile_d(T - 1, 1, last=True)
            copy_eT(T - 1, H - 1)
            row_inverse(T - 1, 1)
            scale_xc(T - 1, 1)

            def bn_affine(n, parts, gamma, beta):
                for c in range(KC):
                    dve.bn_aggr(bnmv[:, c], bnst[:, c, 0:parts].rearrange("p t s -> p (t s)")
                                ).then_inc(bn_mv, 1)
                dve.wait_ge(bn_mv, KC * (n + 1))
                dve.tensor_scalar(bnve[:], bnmv[:, :, 1], BN_EPS, None, ALU.add).then_inc(bn_ve, 1)
                dve.wait_ge(bn_rs, n + 1)
                dve.tensor_tensor(bna[:], vec[:, gamma], bnrs[:], ALU.mult).then_inc(bn_a, 1)
                dve.wait_ge(bn_a, n + 1)
                dve.tensor_tensor(bnt[:], bnmv[:, :, 0], bna[:], ALU.mult).then_inc(bn_t, 1)
                dve.wait_ge(bn_t, n + 1)
                dve.tensor_tensor(bnb[:], vec[:, beta], bnt[:], ALU.subtract).then_inc(bn_b, 1)
                dve.wait_ge(bn_b, n + 1)

            def affine0(buf, done):
                for c in range(NCH):
                    cs = slice(c * CH, (c + 1) * CH)
                    dve.tensor_scalar(buf[:, 0, cs], buf[:, 0, cs], bna[:, 0:1], bnb[:, 0:1], ALU.mult,
                                      ALU.add).then_inc(done, 1)

            dve.wait_ge(xc_stats, KC * T)
            bn_affine(0, T, ENC_G, ENC_B)
            affine0(xc, xn0_ready)
            for n in range(KC * NCH):
                f, c = n % KC, n // KC
                cs = slice(c * CH, (c + 1) * CH)
                dve.wait_ge(z_exp, n + 1)
                if f == 0:
                    dve.wait_ge(xn0_ready, c + 1)
                else:
                    dve.wait_ge(xn1_ready, c + 1)
                dve.scalar_tensor_tensor(et[:, 4 + n % 2], et[:, n % 2], 1.0, xc[:, f, cs], ALU.min, ALU.add
                                         ).then_inc(z_t, 1)
                dve.wait_ge(z_relu, n + 1)
                dve.wait_ge(z_t, n + 1)
                dve.scalar_tensor_tensor(hb[:, f, cs], et[:, 2 + n % 2], -1.0, et[:, 4 + n % 2], ALU.add,
                                         ALU.add).then_inc(hb_ready, 1)
                dve.wait_ge(hb_ready, n + 1)
                dve.bn_stats(bnst[:, f, c], hb[:, f, cs]).then_inc(hb_stats, 1)
            dve.wait_ge(hb_stats, KC * NCH)
            bn_affine(1, NCH, EMLP_G, EMLP_BETA)
            affine0(hb, hbn0_ready)
            for n in range(0, T // 2, 2):
                dve.wait_ge(embT_filled, n + 1)
                dve.tensor_copy(emb[:, 2 * n:2 * n + 2], bank[n % 4][:].rearrange("p (t d) -> p t d", t=2)
                                ).then_inc(emb_dve, 1)

            def scale_y(n, tile, c):
                dve.wait_ge(y_done, KC * n + c + 1)
                wait(dve, yw_done, n)
                dve.tensor_tensor(yt[:, c], bank[c][:, 0:P], rb[:, c, tile_cols(tile)], ALU.mult
                                  ).then_inc(yt_ready, 1)

            def elu(n):
                dve.wait_ge(e1_ready, n + 1)
                dve.tensor_scalar(t1[:], e1[:], 1.0, -1.0, ALU.min, ALU.add).then_inc(t1_ready, 1)
                wait(dve, zd_done, n)
                dve.wait_ge(t1_ready, n + 1)
                dve.scalar_tensor_tensor(yc[:], bank[2][:, 0:D].rearrange("p (c n) -> p c n", c=KC), 0.0,
                                         t1[:], ALU.max, ALU.add).then_inc(yc_ready, 1)

            def mlp_out(n, tile):
                dve.wait_ge(zd_exp, n + 1)
                dve.scalar_tensor_tensor(t2[:], e2[:], 1.0, yc[:], ALU.min, ALU.add).then_inc(t2_ready, 1)
                dve.wait_ge(t2_ready, n + 1)
                dve.scalar_tensor_tensor(hd[:, :, tile_cols(tile)], r2[:], -1.0, t2[:], ALU.add, ALU.add
                                         ).then_inc(hd_ready, 1)
                dve.wait_ge(hd_ready, n + 1)
                for c in range(KC):
                    dve.bn_stats(bnst[:, c, tile_row(tile)].rearrange("p o s -> p (o s)"),
                                 hd[:, c, tile_cols(tile)]).then_inc(hd_stats, 1)

            scale_y(0, T - 1, 0)
            scale_y(0, T - 1, 1)

            def step_f(n, tile, before):
                scale_y(n, tile, 0)
                elu(n - 1)
                scale_y(n, tile, 1)
                mlp_out(n - 1, before)

            step_f(1, 0, T - 1)
            step_f(2, 1, 0)
            step_f(3, 2, 1)
            with dve.Fori(1, (T - 1) // 3) as r:
                for b in range(3):
                    step_f(3 * r + b + 1, 3 * r + b, 3 * r + b - 1)
            elu(T - 1)
            mlp_out(T - 1, T - 2)

            dve.wait_ge(hd_stats, KC * T)
            bn_affine(2, T, DMLP_G, DMLP_BETA)
            affine0(hd, hdn0_ready)
            for n in range(T // 2):
                dve.wait_ge(oT_filled, n + 1)
                dve.tensor_tensor(ob[:, 2 * n:2 * n + 2], bank[4 + n % 4][:].rearrange("p (t d) -> p t d", t=2),
                                  x_sb[:, 2 * n:2 * n + 2], ALU.add).then_inc(o_ready, 1)


def kernel(**inputs):
    import numpy as np
    import concourse.bacc as bacc
    from concourse.bass_utils import run_bass_kernel_spmd

    a = {k: np.asarray(v) for k, v in inputs.items()}
    names = ["L0_gnn_bq", "L0_gnn_bk", "L1_gnn_enc_bn_gamma", "L1_gnn_enc_bn_beta", "L1_gnn_enc_mlp_b",
             "L1_gnn_enc_mlp_bn_gamma", "L1_gnn_enc_mlp_bn_beta", "L1_gnn_dec_mlp_b",
             "L1_gnn_dec_mlp_bn_gamma", "L1_gnn_dec_mlp_bn_beta"]
    arrays = {
        "x": a["x"],
        "adj": a["adj"],
        "wqT": a["L0_gnn_Wq"].T,
        "wkT": a["L0_gnn_Wk"].T,
        "wvT": a["L0_gnn_Wv"].T,
        "bv": a["L0_gnn_bv"],
        "cols": np.stack([a[n] for n in names]).reshape(len(names), -1, P).transpose(2, 0, 1),
        "w_head": a["L1_gnn_W"],
        "w_headT": a["L1_gnn_W"].transpose(0, 2, 1),
        "v_head": a["L1_gnn_V"][..., 0].transpose(0, 2, 1),
        "enc_wT": a["L1_gnn_enc_mlp_W"].T,
        "dec_wT": a["L1_gnn_dec_mlp_W"].T,
    }
    arrays = {f"in_{k}": np.ascontiguousarray(v) for k, v in arrays.items()}
    nc = bacc.Bacc("TRN2", target_bir_lowering=False, num_devices=1, dynamic_dma_scratch_size=KIB)
    args = [nc.dram_tensor(k, v.shape, mybir.dt.from_np(v.dtype), kind="ExternalInput").ap()
            for k, v in arrays.items()]
    out = nc.dram_tensor("out", a["x"].shape, mybir.dt.from_np(a["x"].dtype), kind="ExternalOutput").ap()
    build(nc, *args, out)
    r = run_bass_kernel_spmd(nc, [arrays], core_ids=[0])
    return r.results[0]["out"]
```

```python
from contextlib import ExitStack

import concourse.bass as bass
from concourse import mybir

ALU = mybir.AluOpType
ACT = mybir.ActivationFunctionType
AX_X = mybir.AxisListType.X
F32 = mybir.dt.float32
F32R = mybir.dt.float32r

P = 128
KIB = 1024
BIG = 1.0e36
ROW_FLOOR = -1.0e27
ABOVE_ONE = 1.0 + 2.0 ** -23
LN_EPS = 1e-5
BN_EPS = 1e-6

BQ, BK, ENC_G, ENC_B, EMLP_B, EMLP_G, EMLP_BETA, DMLP_B, DMLP_G, DMLP_BETA = range(10)


def build(nc, x, adj, wqT, wkT, wvT, bv, cols, w_head, w_headT, v_head, enc_wT, dec_wT, out):
    N, D = x.shape
    H, E, _ = w_head.shape
    T = N // P
    KC = D // P
    CH = 512
    NCH = N // CH
    TPC = CH // P
    assert E * H == D and KC == 2 and H == 4 and T == 16

    adjm_dram = nc.dram_tensor("adjm_dram", [N, N], F32)
    att_dram = nc.dram_tensor("att_dram", [T * H, P, N], F32)

    with ExitStack() as ctx:
        def small(name, shape, dt=F32):
            return ctx.enter_context(nc.sbuf_tensor(name, shape, dt))

        def sem(name):
            return ctx.enter_context(nc.semaphore(name))

        ident = small("ident", [P, P])
        vec = small("vec", [P, 10, KC])
        bq_s = small("bq_s", [P, KC])
        neg_half = small("neg_half", [P, T])
        wx = small("wx", [P, KC, P + 4])
        wTbd = small("wTbd", [P, KC, P])
        vbd = small("vbd", [P, KC, 4])
        fnat = small("fnat", [P, T, 2 * H])
        stats1 = small("stats1", [P, 6])
        mv1 = small("mv1", [P, T, 2])
        veps = small("veps", [P, T])
        rstd1 = small("rstd1", [P, T])
        cmax = small("cmax", [P, 2, NCH])
        rmax = small("rmax", [P, 2])
        negm = small("negm", [P, 2])
        rsum = small("rsum", [P, 2])
        rinv = small("rinv", [P, 1])
        mv2 = small("mv2", [P, 2])
        veps2 = small("veps2", [P, 1])
        rstd2 = small("rstd2", [P, 1])
        fcur = small("fcur", [P, 2, H])
        hmax = small("hmax", [P, 2, H])
        hneg = small("hneg", [P, 2, H])
        hsum = small("hsum", [P, 2, H])
        hval = small("hval", [P, H])
        hrec = small("hrec", [P, H])
        hinv = small("hinv", [P, H, E])
        bnst = small("bnst", [P, KC, T, 6])
        bnmv = small("bnmv", [P, KC, 2])
        bnve = small("bnve", [P, KC])
        bnrs = small("bnrs", [P, KC])
        bna = small("bna", [P, KC])
        bnt = small("bnt", [P, KC])
        bnb = small("bnb", [P, KC])
        scratch = small("scratch", [P, 5, D])
        xt, hn = scratch[:, 0], scratch[:, 1]
        yb = wx[:, :, 0:P]
        h2T = scratch[:, 2].rearrange("p (c n) -> p c n", c=KC)
        yt, yc, e1, e2, r2 = [scratch[:, n].rearrange("p (c n) -> p c n", c=KC) for n in range(5)]

        base = 16 * KIB
        def at(name, shape, kib, dt=F32):
            return nc.alloc_sbuf_tensor_at(name, shape, dt, offset=base + kib * KIB)

        x_sb = at("x_sb", [P, T, D], 0)
        xw = at("xw", [P, T, D], 16)
        hn_all = at("hn_all", [P, T, D], 16)
        hb = at("hb", [P, KC, N], 16)
        qhl = at("qhl", [P, 2 * KC, N], 32, F32R)
        khl = at("khl", [P, 2 * KC, N], 64, F32R)
        vhl = at("vhl", [P, T, 2 * D], 96, F32R)
        f2b = at("f2b", [P, H, N], 32)
        eb = at("eb", [P, H, N], 64)
        att = at("att", [P, H, N], 96)
        ring = [[at(f"ring{b}{c}", [P, 2, N], kib) for c, kib in enumerate(where)]
                for b, where in enumerate(((96, 112), (64, 80), (32, 48), (128, 144)))]
        adjt = at("adjt", [P, 2, N], 128)
        sc = at("sc", [P, 2, N], 144)
        hT = at("hT", [P, 2, 2 * KC, CH], 144, F32R)
        xc = at("xc", [P, KC, N], 144)
        hd = at("hd", [P, KC, N], 16)
        msk = at("msk", [P, 2, N], 160)
        whl = at("whl", [P, 3, 2 * KC, D], 160, F32R)
        emb = at("emb", [P, T, D], 160)
        att_hl = at("att_hl", [P, 2, N], 176, F32R)
        wqkv = at("wqkv", [P, 3, KC, D], 176)
        bvb = at("bvb", [P, D], 182)
        rb = at("rb", [P, KC, N], 176)
        et = at("et", [P, 8, CH], 128)
        qcur = at("qcur", [P, 2, 2 * KC, P], -4, F32R)
        wmlp = at("wmlp", [P, 2, KC, D], -4)
        ob = at("ob", [P, T, D], 64)

        bank0 = ctx.enter_context(nc.psum_tensor("bank0", [P, CH], F32))
        banks123 = ctx.enter_context(nc.psum_tensor("banks123", [P, 3, CH], F32))
        banks4567 = ctx.enter_context(nc.psum_tensor("banks4567", [P, 4, CH], F32))
        bank = [bank0[:]] + [banks123[:, b] for b in range(3)] + [banks4567[:, b] for b in range(4)]

        x_in = [sem(f"x_in{g}") for g in range(NCH)]
        weights_in = sem("weights_in")
        heads_in = sem("heads_in")
        adj_in = [sem(f"adj_in{b}") for b in range(2)]
        wmlp_in = sem("wmlp_in")
        const_ready = sem("const_ready")
        bq_ready = sem("bq_ready")
        zeroed = sem("zeroed")
        wv_done = sem("wv_done")
        wx_ready = sem("wx_ready")
        ln1_stats = sem("ln1_stats")
        ln1_mv = sem("ln1_mv")
        ln1_veps = sem("ln1_veps")
        ln1_rstd = sem("ln1_rstd")
        hn_all_ready = sem("hn_all_ready")
        hT_filled = sem("hT_filled")
        hT_headed = sem("hT_headed")
        hT_split = sem("hT_split")
        w_headed = sem("w_headed")
        w_split = sem("w_split")
        bv_added = sem("bv_added")
        proj_done = sem("proj_done")
        proj_headed = sem("proj_headed")
        proj_split = sem("proj_split")

        qcur_ready = sem("qcur_ready")
        scores_ready = sem("scores_ready")
        scores_used = sem("scores_used")
        rmax_ready = sem("rmax_ready")
        negm_ready = sem("negm_ready")
        probs_ready = sem("probs_ready")
        probsT_filled = sem("probsT_filled")
        probsT_head = sem("probsT_head")
        probsT_rest = sem("probsT_rest")
        pv_group = sem("pv_group")
        mask_ready = sem("mask_ready")
        masked = sem("masked")
        adjm_out = [sem(f"adjm_out{b}") for b in range(2)]
        rinv_ready = sem("rinv_ready")
        xt_ready = sem("xt_ready")
        x1_ready = sem("x1_ready")
        ln2_stats = sem("ln2_stats")
        ln2_mv = sem("ln2_mv")
        ln2_veps = sem("ln2_veps")
        ln2_rstd = sem("ln2_rstd")
        hn_ready = sem("hn_ready")
        hnT_filled = sem("hnT_filled")
        h2T_ready = sem("h2T_ready")
        xw_done = sem("xw_done")
        xw_copied = sem("xw_copied")

        f2_filled = sem("f2_filled")
        f2_act = sem("f2_act")
        f2_dve = sem("f2_dve")

        adjm_in = [sem(f"adjm_in{b}") for b in range(2)]
        fcur_ready = sem("fcur_ready")
        tanh_ready = sem("tanh_ready")
        sig_ready = sem("sig_ready")
        hmax_ready = sem("hmax_ready")
        hneg_ready = sem("hneg_ready")
        exp_ready = sem("exp_ready")
        eT_filled = sem("eT_filled")
        attA = sem("attA")
        attB = sem("attB")
        pair_done = sem("pair_done")
        att_out = [sem(f"att_out{h}") for h in range(H)]
        hval_ready = sem("hval_ready")
        hrec_ready = sem("hrec_ready")
        hinv_ready = sem("hinv_ready")
        rbT_filled = sem("rbT_filled")
        rb_ready = sem("rb_ready")
        xc_ready = sem("xc_ready")
        xc_stats = sem("xc_stats")

        bn_mv = sem("bn_mv")
        bn_ve = sem("bn_ve")
        bn_rs = sem("bn_rs")
        bn_a = sem("bn_a")
        bn_t = sem("bn_t")
        bn_b = sem("bn_b")
        xn0_ready = sem("xn0_ready")
        xn1_ready = sem("xn1_ready")
        z_done = sem("z_done")
        z_exp = sem("z_exp")
        z_relu = sem("z_relu")
        z_t = sem("z_t")
        hb_ready = sem("hb_ready")
        hb_stats = sem("hb_stats")
        embT_filled = sem("embT_filled")
        emb_act = sem("emb_act")

        ring_in = [[sem(f"ring_in{b}{c}") for c in range(KC)] for b in range(4)]
        y_done = sem("y_done")
        yb_ready = sem("yb_ready")
        ys_ready = sem("ys_ready")
        yt_ready = sem("yt_ready")
        yw_done = sem("yw_done")
        e1_ready = sem("e1_ready")
        t1_ready = sem("t1_ready")
        yc_ready = sem("yc_ready")
        zd_done = sem("zd_done")
        zd_exp = sem("zd_exp")
        zd_relu = sem("zd_relu")
        t2_ready = sem("t2_ready")
        hd_ready = sem("hd_ready")
        hd_stats = sem("hd_stats")
        hdn0_ready = sem("hdn0_ready")
        hdn1_ready = sem("hdn1_ready")
        oT_filled = sem("oT_filled")
        o_ready = sem("o_ready")
        out_stored = sem("out_stored")
        waits_apart = [sem(f"waits_apart{n}") for n in range(2)]

        block = ctx.enter_context(nc.Block())

        def wait(eng, s, value):
            if not isinstance(value, int) or value > 0:
                eng.wait_ge(s, value)

        def wait_apart(eng, s, value):
            if isinstance(value, int):
                wait(eng, s, value)
            else:
                eng.wait_ge(s, value).then_inc(waits_apart[eng is nc.vector], 1)

        def tile_no(i, count=T):
            if isinstance(i, int):
                return i
            return nc.s_assert_within(i, 0, count - 1, skip_runtime_bounds_check_because="the loop's count is fixed")

        def tile_cols(i):
            return bass.ds(tile_no(i) * P, P)

        def tile_row(i):
            return bass.ds(tile_no(i), 1)

        def loads(i, b):
            return 8 * i + (8 if b else 16)

        LAST = NCH - 1
        F2_PARTS = [(h, g) for h in range(2) for g in range(LAST)] + [(2, 0), (2, 1)]
        F2_EARLY = len(F2_PARTS)
        F2_PARTS += [(0, LAST), (1, LAST), (2, 2), (2, LAST)] + [(3, g) for g in range(NCH)]
        F2_ACT = list(range(F2_EARLY - 1)) + [F2_EARLY]
        F2_DVE = [n for n in range(H * NCH) if n not in F2_ACT]

        PROJ = [(which, f) for which in range(2) for f in range(KC)] + [(2, t) for t in range(TPC)]
        NP = len(PROJ)
        PROJ_BANKS = (0, 1, 2, 3, 6, 7)
        N_WEIGHT_DMAS = 3 + 1 + 1

        @block.sync
        def _(sp):
            for g in range(NCH):
                sp.dma_start(x_sb[:, TPC * g:TPC * (g + 1)],
                             x[g * CH:(g + 1) * CH, :].rearrange("(t p) d -> p t d", p=P)).then_inc(x_in[g], 16)
                if g == 0:
                    for n, w in enumerate((wqT, wkT, wvT)):
                        sp.dma_start(wqkv[:, n], w.rearrange("(c p) d -> p c d", p=P)).then_inc(weights_in, 16)
                    sp.dma_start(vec[:], cols).then_inc(weights_in, 16)
                    sp.dma_start(bvb[:], bv.partition_broadcast(P)).then_inc(weights_in, 16)
            for k in range(2):
                sp.dma_start(adjt[:, k], adj[k * P:(k + 1) * P, :]).then_inc(adj_in[k], 16)
            sp.wait_ge(zeroed, 3)
            for h in range(H):
                c, r = h // 2, E * (h % 2)
                sp.dma_start(wx[r:r + E, c, r:r + E], w_head[h]).then_inc(heads_in, 16)
                sp.dma_start(wTbd[r:r + E, c, r:r + E], w_headT[h]).then_inc(heads_in, 16)
                sp.dma_start(vbd[r:r + E, c, 2 * (h % 2):2 * (h % 2) + 2], v_head[h]).then_inc(heads_in, 16)

            def rows(k, b, more):
                sp.wait_ge(masked, k + 1)
                sp.dma_start(adjm_dram[tile_cols(k), :], msk[:, b]).then_inc(adjm_out[b], 16)
                if more:
                    sp.dma_start(adjt[:, b], adj[tile_cols(k + 2), :]).then_inc(adj_in[b], 16)

            with sp.Fori(0, T - 2, 2) as k:
                for b in range(2):
                    rows(k + b, b, True)
            for b in range(2):
                rows(T - 2 + b, b, False)

            sp.wait_ge(scores_ready, NCH * T)
            for n, w in enumerate((enc_wT, dec_wT)):
                sp.dma_start(wmlp[:, n], w.rearrange("(c p) d -> p c d", p=P)).then_inc(wmlp_in, 16)

            for b in range(2):
                sp.wait_ge(adjm_out[b], 16 * (T // 2))
            sp.dma_start(adjt[:, 0], adjm_dram[0:P, :]).then_inc(adjm_in[0], 16)

            def load_adjm(i, b):
                wait(sp, hmax_ready, H * (i - 1))
                sp.dma_start(adjt[:, b], adjm_dram[tile_cols(i), :]).then_inc(adjm_in[b], 16)

            def store_att(u, h):
                sp.wait_ge(attB, u + 1)
                sp.wait_ge(attA, u + 1)
                sp.dma_start(att_dram[bass.ds(tile_no(u, T * H), 1)].rearrange("o p n -> p (o n)"),
                             att[:, h]).then_inc(att_out[h], 16)

            def spill(i, b, first=False, last=False):
                for h in range(H):
                    if h == 0 and not last:
                        load_adjm(i + 1, 1 - b)
                    if h == 0 and not first:
                        store_att(H * i - 1, H - 1)
                    if h > 0 and not last:
                        store_att(H * i + h - 1, h - 1)

            spill(0, 0, first=True)
            with sp.Fori(1, T - 1, 2) as i:
                spill(i, 1)
                spill(i + 1, 0)
            spill(T - 1, 1, last=True)

            def load_ring(b, tile, c):
                sp.dma_start(ring[b][c][:], att_dram[bass.ds(H * tile_no(tile) + 2 * c, 2)].rearrange("h p n -> p h n")
                             ).then_inc(ring_in[b][c], 16)
            for h in range(H):
                sp.wait_ge(att_out[h], 16 * (T - 1))
            for c in range(KC):
                sp.wait_ge(eT_filled, 2 * H * T)
                load_ring(1, 0, c)
            for c in range(KC):
                sp.wait_ge(tanh_ready, H * T)
                load_ring(2, 1, c)
            for c in range(KC):
                sp.wait_ge(hb_ready, KC * NCH)
                load_ring(3, 2, c)

            def refill(r):
                for b in range(4):
                    for c in range(KC):
                        n = 4 * r + b
                        sp.wait_ge(y_done, KC * (n - 4) + c + 1)
                        load_ring(b, n - 1, c)

            refill(1)
            with sp.Fori(2, T // 4) as r:
                refill(r)

            for n in range(T // 2):
                sp.wait_ge(o_ready, n + 1)
                sp.dma_start(out[2 * n * P:2 * (n + 1) * P, :].rearrange("(t p) d -> p t d", p=P),
                             ob[:, 2 * n:2 * n + 2]).then_inc(out_stored, 16)
            sp.wait_ge(out_stored, 16 * (T // 2))

        @block.gpsimd
        def _(pool):
            pool.memset(wx[:], 0.0).then_inc(zeroed, 1)
            pool.memset(wTbd[:], 0.0).then_inc(zeroed, 1)
            pool.memset(vbd[:], 0.0).then_inc(zeroed, 1)
            pool.memset(neg_half[:], -0.5).then_inc(const_ready, 1)
            pool.memset(ident[:], 0.0).then_inc(const_ready, 1)
            pool.wait_ge(const_ready, 2)
            pool.affine_select(out=ident[:], in_=ident[:], compare_op=ALU.not_equal, fill=1.0,
                               base=0, pattern=[[-1, P]], channel_multiplier=1).then_inc(const_ready, 1)
            for g in range(NCH):
                gs = slice(TPC * g, TPC * (g + 1))
                pool.wait_ge(ln1_veps, g + 1)
                pool.tensor_tensor(rstd1[:, gs], veps[:, gs], neg_half[:, gs], ALU.pow).then_inc(ln1_rstd, 1)
            pool.wait_ge(weights_in, 16 * N_WEIGHT_DMAS)
            for g in range(NCH):
                gs = slice(TPC * g, TPC * (g + 1))
                pool.wait_ge(hn_all_ready, TPC * (g + 1))
                pool.tensor_tensor(x_sb[:, gs], x_sb[:, gs], bvb[:].unsqueeze(1).broadcast_to([P, TPC, D]),
                                   ALU.add).then_inc(bv_added, 1)

            def copy_q(k, b):
                pool.tensor_copy(qcur[:, b], qhl[:, :, tile_cols(k)]).then_inc(qcur_ready, 1)

            pool.wait_ge(proj_split, NP * NCH - TPC)
            copy_q(0, 0)
            copy_q(1, 1)

            def rstd_row():
                pool.tensor_tensor(rstd2[:], veps2[:], neg_half[:, 0:1], ALU.pow).then_inc(ln2_rstd, 1)

            for k in range(2):
                pool.wait_ge(scores_ready, NCH * (k + 1))
                copy_q(k + 2, k)
            with pool.Fori(2, T - 2, 2) as k:
                for b in range(2):
                    pool.wait_ge(ln2_veps, k + b - 1)
                    rstd_row()
                    pool.wait_ge(scores_ready, NCH * (k + b + 1))
                    copy_q(k + b + 2, b)
            for k in range(T - 2, T + 2):
                pool.wait_ge(ln2_veps, k - 1)
                rstd_row()
            def spread_inverse(i):
                pool.wait_ge(hval_ready, i + 1)
                wait(pool, rbT_filled, KC * i)
                pool.wait_ge(hrec_ready, i + 1)
                pool.tensor_tensor(hinv[:], hval[:].unsqueeze(2).broadcast_to([P, H, E]),
                                   hrec[:].unsqueeze(2).broadcast_to([P, H, E]), ALU.mult
                                   ).then_inc(hinv_ready, 1)

            def sigmoid(i, h):
                wait_apart(pool, tanh_ready, H * i + h + 1)
                pool.tensor_scalar(eb[:, h], eb[:, h], ABOVE_ONE, 0.5, ALU.add, ALU.mult).then_inc(sig_ready, 1)

            def negate_max(i, b, h):
                wait_apart(pool, hmax_ready, H * i + h + 1)
                pool.tensor_scalar(hneg[:, b, h:h + 1], hmax[:, b, h:h + 1], -1.0, None, ALU.mult
                                   ).then_inc(hneg_ready, 1)

            def tile_d(i, b, first=False):
                for h in range(H):
                    sigmoid(i, h)
                    if h > 0:
                        negate_max(i, b, h - 1)
                    elif not first:
                        negate_max(i - 1, 1 - b, H - 1)
                    if h == 2 and not first:
                        spread_inverse(i - 1)

            tile_d(0, 0, first=True)
            with pool.Fori(1, T - 1, 2) as i:
                tile_d(i, 1)
                tile_d(i + 1, 0)
            tile_d(T - 1, 1)
            negate_max(T - 1, 1, H - 1)
            spread_inverse(T - 1)
            for n in range(3):
                pool.wait_ge(bn_ve, n + 1)
                pool.tensor_tensor(bnrs[:], bnve[:], neg_half[:, 0:KC], ALU.pow).then_inc(bn_rs, 1)

        @block.scalar
        def _(act):
            act.wait_ge(weights_in, 16 * N_WEIGHT_DMAS)
            act.activation(bq_s[:], vec[:, BQ], ACT.Copy, scale=1.0 / 32).then_inc(bq_ready, 1)
            for which in range(3):
                act.activation(whl[:, which, 0:KC], wqkv[:, which], ACT.Copy,
                               scale=1.0 / 32 if which == 0 else 1.0).then_inc(w_headed, 1)

            def relu_head(g):
                for c in range(KC):
                    act.wait_ge(hT_filled, KC * g + c + 1)
                    wait(act, proj_done, NP * (g - 1))
                    act.activation(hT[:, g % 2, c], bank[4 + c][:], ACT.Relu).then_inc(hT_headed, 1)

            def proj_head(m):
                g, (which, f) = m // NP, PROJ[m % NP]
                src = bank[PROJ_BANKS[m % 6]]
                act.wait_ge(proj_done, m + 1)
                if which < 2:
                    act.activation((qhl, khl)[which][:, f, g * CH:(g + 1) * CH], src, ACT.Identity,
                                   bias=(bq_s, vec[:, BK])[which][:, f:f + 1]).then_inc(proj_headed, 1)
                else:
                    act.activation(vhl[:, TPC * g + f, 0:D], src[:, 0:D], ACT.Copy).then_inc(proj_headed, 1)

            relu_head(0)
            act.wait_ge(bq_ready, 1)
            for m in range(NP * NCH):
                proj_head(m)
                if m % NP == 2 * KC - 1 and m // NP + 1 < NCH:
                    relu_head(m // NP + 1)

            def probs(k, b):
                act.wait_ge(negm_ready, k + 1)
                act.activation(sc[:, b], sc[:, b], ACT.Exp, bias=negm[:, b:b + 1],
                               accum_out=rsum[:, b:b + 1]).then_inc(probs_ready, 1)

            def head(k, g):
                act.wait_ge(probsT_filled, NCH * k + g + 1)
                wait(act, pv_group, NCH * (k - 1) + g + 1)
                act.activation(att_hl[:, 0, g * CH:(g + 1) * CH], bank[4 + g % 2][:], ACT.Copy
                               ).then_inc(probsT_head, 1)

            def relu_hnT(k):
                act.wait_ge(hnT_filled, k + 1)
                act.activation(h2T, bank[7][:, 0:D].rearrange("p (c n) -> p c n", c=KC), ACT.Relu
                               ).then_inc(h2T_ready, 1)

            def copy_xw(k):
                act.wait_ge(xw_done, k + 1)
                both = bank[7][:, 0:KC * (P + 4)].rearrange("p (c n) -> p c n", c=KC)
                act.activation(xw[:, tile_row(k)].rearrange("p o (c n) -> p (o c) n", c=KC),
                               both[:, :, 0:P], ACT.Copy).then_inc(xw_copied, 1)
                act.activation(fnat[:, tile_row(k)].rearrange("p o (c n) -> p (o c) n", c=KC),
                               both[:, :, P:P + 4], ACT.Copy).then_inc(xw_copied, 1)

            def tile_b(k, b, scores=True, transposed=True, norm=True):
                if transposed:
                    head(k - 1, 0)
                if norm:
                    relu_hnT(k - 2)
                if transposed:
                    for g in range(1, NCH):
                        head(k - 1, g)
                if scores:
                    probs(k, b)
                if norm:
                    copy_xw(k - 2)

            tile_b(0, 0, transposed=False, norm=False)
            tile_b(1, 1, norm=False)
            with act.Fori(2, T, 2) as k:
                tile_b(k, 0)
                tile_b(k + 1, 1)
            tile_b(T, 0, scores=False)

            def copy_f2(n):
                h, g = F2_PARTS[n]
                act.wait_ge(f2_filled, n + 1)
                act.activation(f2b[:, h, g * CH:(g + 1) * CH], bank[n % 4], ACT.Copy).then_inc(f2_act, 1)

            for n in F2_ACT[:6]:
                copy_f2(n)
            relu_hnT(T - 1)
            copy_f2(F2_ACT[6])
            copy_xw(T - 1)
            copy_f2(F2_ACT[7])

            def tanh(i, b, h):
                if h == 0:
                    act.wait_ge(fcur_ready, i + 1)
                wait(act, eT_filled, 2 * (H * (i - 1) + h + 1))
                act.activation(eb[:, h], f2b[:, h], ACT.Tanh, bias=fcur[:, b, h:h + 1], scale=0.5
                               ).then_inc(tanh_ready, 1)

            def exp(i, b, h):
                act.wait_ge(hneg_ready, H * i + h + 1)
                act.activation(eb[:, h], eb[:, h], ACT.Exp, bias=hneg[:, b, h:h + 1],
                               accum_out=hsum[:, b, h:h + 1]).then_inc(exp_ready, 1)

            def copy_eT(i, h):
                act.wait_ge(eT_filled, 2 * (H * i + h) + 1)
                wait(act, pair_done, KC * (i - 1) + h // 2 + 1)
                wait(act, att_out[h], 16 * i)
                act.activation(att[:, h, 0:CH], bank[0], ACT.Copy).then_inc(attA, 1)

            def tanh_first(h):
                for copied, parts in ((f2_act, F2_ACT), (f2_dve, F2_DVE)):
                    wait(act, copied, max([m + 1 for m, n in enumerate(parts) if F2_PARTS[n][0] == h], default=0))
                tanh(0, 0, h)

            def tile_d(i, b, first=False, last=False):
                for h in range(H):
                    if h < 2 and first:
                        tanh_first(h + 2)
                    elif h < 2:
                        tanh(i, b, h + 2)
                    elif not last:
                        tanh(i + 1, 1 - b, h - 2)
                    if h > 0:
                        copy_eT(i, h - 1)
                    elif not first:
                        copy_eT(i - 1, H - 1)
                    exp(i, b, h)

            tanh_first(0)
            tanh_first(1)
            tile_d(0, 0, first=True)
            tile_d(1, 1)
            tile_d(2, 0)
            with act.Fori(3, T - 1, 2) as i:
                tile_d(i, 1)
                tile_d(i + 1, 0)
            tile_d(T - 1, 1, last=True)
            copy_eT(T - 1, H - 1)

            act.wait_ge(bn_b, 1)
            for c in range(NCH):
                act.activation(xc[:, 1, c * CH:(c + 1) * CH], xc[:, 1, c * CH:(c + 1) * CH], ACT.Identity,
                               bias=bnb[:, 1:2], scale=bna[:, 1:2]).then_inc(xn1_ready, 1)
            def copy_emb(n):
                act.wait_ge(embT_filled, n + 1)
                act.activation(emb[:, 2 * n:2 * n + 2], bank[4 + n % 4].rearrange("p (t d) -> p t d", t=2),
                               ACT.Copy).then_inc(emb_act, 1)

            for n in range(KC * NCH):
                f = n % KC
                act.wait_ge(z_done, n + 1)
                wait(act, hb_ready, n - 1)
                act.activation(et[:, n % 2], bank[n % 4][:], ACT.Exp, bias=vec[:, EMLP_B, f:f + 1]
                               ).then_inc(z_exp, 1)
                act.activation(et[:, 2 + n % 2], bank[n % 4][:], ACT.Relu, bias=vec[:, EMLP_B, f:f + 1]
                               ).then_inc(z_relu, 1)
                if n >= 4:
                    copy_emb(n - 4)
            for n in range(4, T // 2):
                copy_emb(n)

            def elu_in(n):
                act.wait_ge(yw_done, n + 1)
                act.activation(e1, bank[2][:, 0:D].rearrange("p (c n) -> p c n", c=KC), ACT.Exp
                               ).then_inc(e1_ready, 1)

            def mlp_out(n):
                act.wait_ge(zd_done, n + 1)
                for f in range(KC):
                    act.activation(e2[:, f], bank[3][:, f * P:(f + 1) * P], ACT.Exp,
                                   bias=vec[:, DMLP_B, f:f + 1]).then_inc(zd_exp, 1)
                for f in range(KC):
                    act.activation(r2[:, f], bank[3][:, f * P:(f + 1) * P], ACT.Relu,
                                   bias=vec[:, DMLP_B, f:f + 1]).then_inc(zd_relu, 1)

            def step_f(n):
                wait(act, yc_ready, n - 1)
                elu_in(n - 1)
                wait(act, hd_ready, n - 1)
                mlp_out(n - 1)

            step_f(1)
            with act.Fori(2, T + 1) as n:
                step_f(n)

            act.wait_ge(bn_b, 3)
            for c in range(NCH):
                act.activation(hd[:, 1, c * CH:(c + 1) * CH], hd[:, 1, c * CH:(c + 1) * CH], ACT.Identity,
                               bias=bnb[:, 1:2], scale=bna[:, 1:2]).then_inc(hdn1_ready, 1)

        @block.tensor
        def _(pe):
            def keep_warm(count, free):
                for _ in range(count):
                    pe.transpose(free[:, 0:P], ident[:], ident[:])

            PRODUCTS = ((0, 0), (0, 1), (1, 0))

            def transpose_h(g):
                for c in range(KC):
                    wait(pe, hT_split, KC * (g - 1) + c + 1)
                    pe.wait_ge(hn_all_ready, TPC * (g + 1))
                    for t in range(TPC):
                        last = pe.transpose(bank[4 + c][:, t * P:(t + 1) * P],
                                            hn_all[:, TPC * g + t, c * P:(c + 1) * P], ident[:])
                    last.then_inc(hT_filled, 1)

            pe.wait_ge(const_ready, 3)
            keep_warm(18, bank[7])
            transpose_h(0)
            keep_warm(8, bank[7])
            pe.wait_ge(w_split, 3)
            for m in range(NP * NCH):
                g, (which, f) = m // NP, PROJ[m % NP]
                dst = bank[PROJ_BANKS[m % 6]]
                if m % NP == 0:
                    pe.wait_ge(hT_split, KC * (g + 1))
                wait(pe, proj_split, m - 5)
                for n, (a, z) in enumerate(PRODUCTS):
                    for c in range(KC):
                        if which < 2:
                            w, h = whl[:, which, KC * a + c, f * P:(f + 1) * P], hT[:, g % 2, KC * z + c]
                            last = pe.matmul(dst, w, h, start=(n == c == 0), stop=(n == 2 and c == KC - 1))
                        else:
                            h, w = hT[:, g % 2, KC * a + c, f * P:(f + 1) * P], whl[:, 2, KC * z + c]
                            last = pe.matmul(dst[:, 0:D], h, w, start=(n == c == 0), stop=(n == 2 and c == KC - 1))
                last.then_inc(proj_done, 1)
                if m % NP == 2 * KC - 1 and g + 1 < NCH:
                    transpose_h(g + 1)
            pe.wait_ge(heads_in, 16 * 3 * H)
            pe.wait_ge(proj_split, NP * NCH)
            for c in range(KC):
                last = pe.matmul(bank[7][:, 4 * c:4 * c + 4], wTbd[:, c], vbd[:, c])
            last.then_inc(wv_done, 1)

            def scores(k, b, chunks):
                pe.wait_ge(qcur_ready, k + 1)
                for n in chunks:
                    wait(pe, scores_used, NCH * (k - 1) + n + 1)
                    for c in range(KC):
                        for a, z in ((0, 0), (0, KC), (KC, 0)):
                            last = pe.matmul(bank[n][:], qcur[:, b, a + c], khl[:, z + c, n * CH:(n + 1) * CH],
                                             start=(c == 0 and a == z), stop=(c == KC - 1 and a > 0))
                    last.then_inc(scores_ready, 1)

            def transpose_probs(k, b, g):
                if g == 0:
                    pe.wait_ge(probs_ready, k + 1)
                wait(pe, probsT_rest, NCH * k + g - 1)
                for t in range(TPC):
                    last = pe.transpose(bank[4 + g % 2][:, t * P:(t + 1) * P],
                                        sc[:, b, g * CH + t * P:g * CH + (t + 1) * P], ident[:])
                last.then_inc(probsT_filled, 1)

            def attend(k, g):
                pv = bank[6]
                if g == 0:
                    wait(pe, x1_ready, k)
                jobs = [(0, t) for t in range(TPC)] + [(1, t) for t in range(TPC)]
                if g == NCH - 1:
                    jobs = jobs[:TPC - 1] + jobs[TPC:] + [jobs[TPC - 1]]
                for n, (part, t) in enumerate(jobs):
                    if n == 0:
                        pe.wait_ge(probsT_head, NCH * k + g + 1)
                    if part == 1 and t == 0:
                        pe.wait_ge(probsT_rest, NCH * k + g + 1)
                    j = TPC * g + t
                    width = D if part else 2 * D
                    last = pe.matmul(pv[:, 0:width], att_hl[:, part, j * P:(j + 1) * P], vhl[:, j, 0:width],
                                     start=(g == 0 and n == 0), stop=(g == NCH - 1 and n == 2 * TPC - 1))
                last.then_inc(pv_group, 1)

            def transpose_hn(k):
                pe.wait_ge(hn_ready, k + 1)
                wait(pe, xw_copied, 2 * k)
                for c in range(KC):
                    last = pe.transpose(bank[7][:, c * P:(c + 1) * P], hn[:, c * P:(c + 1) * P], ident[:])
                last.then_inc(hnT_filled, 1)

            def project_w(k):
                if isinstance(k, int) and k == 0:
                    pe.wait_ge(wx_ready, 1)
                pe.wait_ge(h2T_ready, k + 1)
                for c in range(KC):
                    last = pe.matmul(bank[7][:, c * (P + 4):(c + 1) * (P + 4)], h2T[:, c], wx[:, c])
                last.then_inc(xw_done, 1)

            def tile_b(k, b, scored=True, attended=True, norm=True):
                if scored:
                    scores(k, b, range(NCH - 1))
                if attended:
                    transpose_probs(k - 1, 1 - b, 0)
                if scored:
                    scores(k, b, range(NCH - 1, NCH))
                if norm and scored:
                    transpose_hn(k - 2)
                if attended:
                    for g in range(NCH):
                        if g + 1 < NCH:
                            transpose_probs(k - 1, 1 - b, g + 1)
                        if g == 0 and not scored:
                            transpose_hn(k - 2)
                        attend(k - 1, g)
                if norm and not (scored or attended):
                    transpose_hn(k - 2)
                if norm:
                    project_w(k - 2)

            tile_b(0, 0, attended=False, norm=False)
            tile_b(1, 1, norm=False)
            tile_b(2, 0)
            tile_b(3, 1)
            with pe.Fori(4, T, 2) as k:
                tile_b(k, 0)
                tile_b(k + 1, 1)
            tile_b(T, 0, scored=False)

            def spread_f2(n):
                h, g = F2_PARTS[n]
                if n >= 4:
                    if n - 4 in F2_ACT:
                        pe.wait_ge(f2_act, F2_ACT.index(n - 4) + 1)
                    else:
                        pe.wait_ge(f2_dve, F2_DVE.index(n - 4) + 1)
                for t in range(TPC):
                    last = pe.transpose(bank[n % 4][:, t * P:(t + 1) * P],
                                        fnat[:, TPC * g + t, 2 * h + 1:2 * h + 2].broadcast_to([P, P]), ident[:])
                last.then_inc(f2_filled, 1)

            pe.wait_ge(scores_used, NCH * T)
            pe.wait_ge(xw_copied, 2 * TPC * (NCH - 1))
            for n in range(6):
                spread_f2(n)
            transpose_hn(T - 1)
            spread_f2(6)
            project_w(T - 1)
            spread_f2(7)
            pe.wait_ge(xw_copied, 2 * T)
            for n in range(F2_EARLY, H * NCH):
                spread_f2(n)

            def transpose_e(i, h):
                pe.wait_ge(exp_ready, H * i + h + 1)
                u = H * i + h
                for n in range(NCH):
                    if n == 0:
                        wait(pe, attA, u)
                    elif n == 1:
                        wait(pe, attB, u)
                    for t in range(TPC):
                        j = TPC * n + t
                        last = pe.transpose(bank[n][:, t * P:(t + 1) * P], eb[:, h, j * P:(j + 1) * P], ident[:])
                    if n in (0, NCH - 1):
                        last.then_inc(eT_filled, 1)

            def attend_pair(i, b, c, half):
                if half == 0:
                    u = H * i + 2 * c + 2
                    pe.wait_ge(attA, u)
                    pe.wait_ge(attB, u)
                    wait(pe, xc_ready, i - 1)
                for j in range(half * T // 2, (half + 1) * T // 2):
                    for m in range(2):
                        h = 2 * c + m
                        last = pe.matmul(bank[4 + KC * b + c][m * E:(m + 1) * E, 0:P],
                                         xw[:, j, h * E:(h + 1) * E], att[:, h, j * P:(j + 1) * P],
                                         start=(j == 0), stop=(j == T - 1))
                if half:
                    last.then_inc(pair_done, 1)

            def spread_rinv(i, b):
                pe.wait_ge(hinv_ready, i + 1)
                for c in range(KC):
                    pe.transpose(bank[4 + KC * b + c][:, P:2 * P],
                                 hinv[:, 2 * c:2 * c + 2].rearrange("p h e -> p (h e)"), ident[:]
                                 ).then_inc(rbT_filled, 1)

            def tile_d(i, b, first=False):
                if not first:
                    transpose_e(i - 1, 3)
                    attend_pair(i - 1, 1 - b, 0, 1)
                transpose_e(i, 0)
                if not first:
                    attend_pair(i - 1, 1 - b, 1, 0)
                transpose_e(i, 1)
                if not first:
                    attend_pair(i - 1, 1 - b, 1, 1)
                    spread_rinv(i - 1, 1 - b)
                transpose_e(i, 2)
                attend_pair(i, b, 0, 0)

            pe.wait_ge(f2_act, len(F2_ACT))
            pe.wait_ge(f2_dve, len(F2_DVE))
            tile_d(0, 0, first=True)
            tile_d(1, 1)
            tile_d(2, 0)
            with pe.Fori(3, T - 1, 2) as i:
                tile_d(i, 1)
                tile_d(i + 1, 0)
            tile_d(T - 1, 1)
            transpose_e(T - 1, 3)
            attend_pair(T - 1, 1, 0, 1)
            attend_pair(T - 1, 1, 1, 0)
            attend_pair(T - 1, 1, 1, 1)
            spread_rinv(T - 1, 1)

            keep_warm(40, bank[0])
            pe.wait_ge(wmlp_in, 32)
            def mlp_enc(n):
                c, f = n // KC, n % KC
                pe.wait_ge(xn0_ready, c + 1)
                pe.wait_ge(xn1_ready, c + 1)
                wait(pe, z_relu, n - 3)
                for a in range(KC):
                    last = pe.matmul(bank[n % 4][:], wmlp[:, 0, a, f * P:(f + 1) * P],
                                     xc[:, a, c * CH:(c + 1) * CH], start=(a == 0), stop=(a == KC - 1))
                last.then_inc(z_done, 1)

            def transpose_emb(n):
                pe.wait_ge(hb_ready, KC * (2 * n // TPC + 1))
                wait(pe, emb_act, n - 3)
                for t in range(2):
                    for a in range(KC):
                        j = 2 * n + t
                        last = pe.transpose(bank[4 + n % 4][:, t * D + a * P:t * D + (a + 1) * P],
                                            hb[:, a, j * P:(j + 1) * P], ident[:])
                last.then_inc(embT_filled, 1)

            for n in range(KC * NCH):
                mlp_enc(n)
                if n >= 4:
                    transpose_emb(n - 4)
            for n in range(4, T // 2):
                transpose_emb(n)

            def attend_emb(n, src, c):
                wait(pe, yt_ready, KC * (n - 1) + c + 1)
                for j in range(T):
                    for m in range(2):
                        h = 2 * c + m
                        last = pe.matmul(bank[c][m * E:(m + 1) * E, 0:P], emb[:, j, h * E:(h + 1) * E],
                                         src[:, m, j * P:(j + 1) * P], start=(j == 0), stop=(j == T - 1))
                last.then_inc(y_done, 1)

            def times_w(n):
                pe.wait_ge(yt_ready, KC * (n + 1))
                wait(pe, yc_ready, n)
                for c in range(KC):
                    last = pe.matmul(bank[2][:, c * P:(c + 1) * P], wTbd[:, c], yt[:, c])
                last.then_inc(yw_done, 1)

            def mlp(n):
                pe.wait_ge(yc_ready, n + 1)
                wait(pe, zd_relu, KC * n)
                for f in range(KC):
                    for a in range(KC):
                        last = pe.matmul(bank[3][:, f * P:(f + 1) * P], wmlp[:, 1, a, f * P:(f + 1) * P],
                                         yc[:, a], start=(a == 0), stop=(a == KC - 1))
                last.then_inc(zd_done, 1)

            pe.wait_ge(emb_act, T // 2)
            attend_emb(0, att[:, 0:2], 0)
            attend_emb(0, att[:, 2:4], 1)

            def step(n, b, loads):
                pe.wait_ge(ring_in[b][0], 16 * loads)
                attend_emb(n, ring[b][0], 0)
                times_w(n - 1)
                pe.wait_ge(ring_in[b][1], 16 * loads)
                attend_emb(n, ring[b][1], 1)
                mlp(n - 1)

            for b in range(1, 4):
                step(b, b, 1)
            with pe.Fori(1, T // 4) as r:
                for b in range(4):
                    step(4 * r + b, b, r + (1 if b else 0))
            times_w(T - 1)
            mlp(T - 1)

            keep_warm(32, bank[7])
            for n in range(T // 2):
                c = 2 * n // TPC
                pe.wait_ge(hdn0_ready, c + 1)
                pe.wait_ge(hdn1_ready, c + 1)
                wait(pe, o_ready, n - 3)
                for t in range(2):
                    for a in range(KC):
                        j = 2 * n + t
                        last = pe.transpose(bank[4 + n % 4][:, t * D + a * P:t * D + (a + 1) * P],
                                            hd[:, a, j * P:(j + 1) * P], ident[:])
                last.then_inc(oT_filled, 1)

        @block.vector
        def _(dve):
            def row_stats(g):
                gs = slice(TPC * g, TPC * (g + 1))
                dve.wait_ge(x_in[g], 16)
                for t in range(TPC * g, TPC * (g + 1)):
                    dve.bn_stats(bnst[:, 0, t], x_sb[:, t]).then_inc(ln1_stats, 1)
                for t in range(TPC * g, TPC * (g + 1)):
                    dve.wait_ge(ln1_stats, t + 1)
                    dve.bn_aggr(mv1[:, t], bnst[:, 0, t]).then_inc(ln1_mv, 1)
                dve.wait_ge(ln1_mv, TPC * (g + 1))
                dve.tensor_scalar(veps[:, gs], mv1[:, gs, 1], LN_EPS, None, ALU.add).then_inc(ln1_veps, 1)

            def normalise_rows(g):
                dve.wait_ge(ln1_rstd, g + 1)
                for t in range(TPC * g, TPC * (g + 1)):
                    dve.tensor_scalar(hn_all[:, t], x_sb[:, t], mv1[:, t, 0:1], rstd1[:, t:t + 1],
                                      ALU.subtract, ALU.mult).then_inc(hn_all_ready, 1)

            def relu_rest(g):
                for c in range(KC):
                    dve.wait_ge(hT_headed, KC * g + c + 1)
                    dve.scalar_tensor_tensor(hT[:, g % 2, KC + c], bank[4 + c][:], 0.0,
                                             hT[:, g % 2, c].bitcast(F32), ALU.max, ALU.subtract
                                             ).then_inc(hT_split, 1)

            def proj_rest(m):
                g, (which, f) = m // NP, PROJ[m % NP]
                src = bank[PROJ_BANKS[m % 6]]
                dve.wait_ge(proj_headed, m + 1)
                if which < 2:
                    dst, cs = (qhl, khl)[which], slice(g * CH, (g + 1) * CH)
                    dve.scalar_tensor_tensor(dst[:, KC + f, cs], src, (bq_s, vec[:, BK])[which][:, f:f + 1],
                                             dst[:, f, cs].bitcast(F32), ALU.add, ALU.subtract
                                             ).then_inc(proj_split, 1)
                else:
                    nv = TPC * g + f
                    dve.tensor_tensor(vhl[:, nv, D:2 * D], src[:, 0:D], vhl[:, nv, 0:D].bitcast(F32),
                                      ALU.subtract).then_inc(proj_split, 1)

            row_stats(0)
            normalise_rows(0)
            for which in range(3):
                dve.wait_ge(w_headed, which + 1)
                dve.scalar_tensor_tensor(whl[:, which, KC:2 * KC], wqkv[:, which],
                                         1.0 / 32 if which == 0 else 1.0,
                                         whl[:, which, 0:KC].bitcast(F32), ALU.mult, ALU.subtract
                                         ).then_inc(w_split, 1)
            relu_rest(0)
            row_stats(1)
            normalise_rows(1)
            for m in range(NP * NCH):
                g = m // NP
                proj_rest(m)
                if m % NP == 0 and g + 2 < NCH:
                    row_stats(g + 2)
                if m % NP == 2 * KC - 1 and g + 1 < NCH:
                    relu_rest(g + 1)
                if m % NP == NP - 1 and g + 2 < NCH:
                    normalise_rows(g + 2)
            dve.wait_ge(heads_in, 16 * 3 * H)
            dve.wait_ge(wv_done, 1)
            dve.tensor_copy(wx[:, :, P:P + 4], bank[7][:, 0:4 * KC].rearrange("p (c k) -> p c k", c=KC)
                            ).then_inc(wx_ready, 1)
            dve.wait_ge(bv_added, NCH)

            def score_rows(k, b, n):
                wait_apart(dve, scores_ready, NCH * k + n + 1)
                if n == 0:
                    wait_apart(dve, adj_in[b], loads(k, b))
                    wait_apart(dve, probsT_filled, NCH * (k - 1))
                cs = slice(n * CH, (n + 1) * CH)
                dve.tensor_tensor_reduce(sc[:, b, cs], bank[n][:], adjt[:, b, cs], 2.0, -3.0e38, ALU.add,
                                         ALU.max, cmax[:, b, n:n + 1]).then_inc(scores_used, 1)

            def row_max(k, b):
                dve.wait_ge(scores_used, NCH * (k + 1))
                dve.tensor_reduce(rmax[:, b:b + 1], cmax[:, b], AX_X, ALU.max).then_inc(rmax_ready, 1)
                dve.wait_ge(rmax_ready, k + 1)
                dve.tensor_scalar(negm[:, b:b + 1], rmax[:, b:b + 1], -1.0, None, ALU.mult
                                  ).then_inc(negm_ready, 1)

            def rest(k, g):
                dve.wait_ge(probsT_head, NCH * k + g + 1)
                wait(dve, pv_group, NCH * (k - 1) + g + 1)
                cs = slice(g * CH, (g + 1) * CH)
                dve.tensor_tensor(att_hl[:, 1, cs], bank[4 + g % 2][:], att_hl[:, 0, cs].bitcast(F32),
                                  ALU.subtract).then_inc(probsT_rest, 1)

            def mask_zero(k, b):
                wait(dve, adjm_out[b], loads(k, b) - 16)
                dve.tensor_scalar(msk[:, b], adjt[:, b], 0.0, -BIG, ALU.is_equal, ALU.mult
                                  ).then_inc(mask_ready, 1)

            def mask_add(k, b):
                dve.wait_ge(mask_ready, k + 1)
                dve.tensor_tensor(msk[:, b], msk[:, b], adjt[:, b], ALU.add).then_inc(masked, 1)

            def residual(k, b):
                row = x_sb[:, tile_row(k)].rearrange("p o d -> p (o d)")
                dve.wait_ge(pv_group, NCH * (k + 1))
                dve.reciprocal(rinv[:], rsum[:, b:b + 1]).then_inc(rinv_ready, 1)
                dve.wait_ge(rinv_ready, k + 1)
                dve.scalar_tensor_tensor(xt, bank[6][:, 0:D], rinv[:], row, ALU.mult, ALU.add
                                         ).then_inc(xt_ready, 1)
                dve.wait_ge(xt_ready, k + 1)
                dve.scalar_tensor_tensor(row, bank[6][:, D:2 * D], rinv[:], xt, ALU.mult, ALU.add
                                         ).then_inc(x1_ready, 1)
                wait_apart(dve, x1_ready, k + 1)
                dve.bn_stats(stats1[:], row).then_inc(ln2_stats, 1)
                wait_apart(dve, ln2_stats, k + 1)
                dve.bn_aggr(mv2[:], stats1[:]).then_inc(ln2_mv, 1)
                dve.wait_ge(ln2_mv, k + 1)
                dve.tensor_scalar(veps2[:], mv2[:, 1:2], LN_EPS, None, ALU.add).then_inc(ln2_veps, 1)

            def normalise(k):
                dve.wait_ge(ln2_rstd, k + 1)
                wait(dve, hnT_filled, k)
                dve.tensor_scalar(hn, x_sb[:, tile_row(k)].rearrange("p o d -> p (o d)"), mv2[:, 0:1],
                                  rstd2[:], ALU.subtract, ALU.mult).then_inc(hn_ready, 1)

            def tile_b(k, b, scored=True, attended=True, norm=True):
                if norm:
                    residual(k - 2, b)
                if scored:
                    score_rows(k, b, 0)
                if norm:
                    normalise(k - 2)
                if scored:
                    for n in range(1, NCH - 1):
                        score_rows(k, b, n)
                if attended:
                    rest(k - 1, 0)
                if scored:
                    score_rows(k, b, NCH - 1)
                    row_max(k, b)
                if attended:
                    rest(k - 1, 1)
                if scored:
                    mask_zero(k, b)
                if attended:
                    rest(k - 1, 2)
                    rest(k - 1, 3)
                if scored:
                    mask_add(k, b)

            tile_b(0, 0, attended=False, norm=False)
            tile_b(1, 1, norm=False)
            tile_b(2, 0)
            tile_b(3, 1)
            with dve.Fori(4, T, 2) as k:
                tile_b(k, 0)
                tile_b(k + 1, 1)
            tile_b(T, 0, scored=False)
            tile_b(T + 1, 1, scored=False, attended=False)

            def bias(i, b):
                wait(dve, tanh_ready, H * (i - 1))
                f1 = fnat[:, tile_row(i)].rearrange("p o (h k) -> p (o h) k", k=2)[:, :, 0]
                dve.tensor_scalar(fcur[:, b], f1, 0.5, None, ALU.mult).then_inc(fcur_ready, 1)

            dve.wait_ge(xw_copied, 2)
            bias(0, 0)
            for n in F2_DVE:
                h, g = F2_PARTS[n]
                dve.wait_ge(f2_filled, n + 1)
                dve.tensor_copy(f2b[:, h, g * CH:(g + 1) * CH], bank[n % 4]).then_inc(f2_dve, 1)

            def head_max(i, b, h):
                if h == 0:
                    wait_apart(dve, adjm_in[b], loads(i, b))
                wait_apart(dve, sig_ready, H * i + h + 1)
                dve.tensor_tensor_reduce(eb[:, h], eb[:, h], adjt[:, b], 1.0, -3.0e38, ALU.mult, ALU.max,
                                         hmax[:, b, h:h + 1]).then_inc(hmax_ready, 1)

            def copy_eT(i, h):
                dve.wait_ge(eT_filled, 2 * (H * i + h) + 2)
                wait(dve, pair_done, KC * (i - 1) + h // 2 + 1)
                wait(dve, att_out[h], 16 * i)
                dve.tensor_copy(att[:, h, CH:4 * CH].rearrange("p (b n) -> p b n", b=3), banks123[:]
                                ).then_inc(attB, 1)

            def row_inverse(i, b):
                dve.wait_ge(exp_ready, H * (i + 1))
                wait(dve, hinv_ready, i)
                dve.tensor_scalar(hval[:], hmax[:, b], ROW_FLOOR, None, ALU.is_gt).then_inc(hval_ready, 1)
                dve.reciprocal(hrec[:], hsum[:, b]).then_inc(hrec_ready, 1)

            def copy_rb(i, b):
                dve.wait_ge(rbT_filled, KC * (i + 1))
                dve.tensor_copy(rb[:, :, tile_cols(i)], banks4567[:, KC * b:KC * (b + 1), P:2 * P]
                                ).then_inc(rb_ready, 1)

            def scale_xc(i, b):
                dve.wait_ge(rb_ready, i + 1)
                dve.wait_ge(pair_done, KC * (i + 1))
                dve.tensor_tensor(xc[:, :, tile_cols(i)], banks4567[:, KC * b:KC * (b + 1), 0:P],
                                  rb[:, :, tile_cols(i)], ALU.mult).then_inc(xc_ready, 1)

            def stats_xc(i):
                for c in range(KC):
                    wait_apart(dve, xc_ready, i + 1)
                    dve.bn_stats(bnst[:, c, tile_row(i)].rearrange("p o s -> p (o s)"),
                                 xc[:, c, tile_cols(i)]).then_inc(xc_stats, 1)

            def tile_d(i, b, first=False, last=False):
                for h in range(H):
                    ahead = (i, b, h + 1) if h + 1 < H else (i + 1, 1 - b, 0)
                    more = h + 1 < H or not last
                    if h == 0 and not last:
                        bias(i + 1, 1 - b)
                    if more:
                        head_max(*ahead)
                    if h == 3 and not first:
                        copy_rb(i - 1, 1 - b)
                    if h > 0:
                        copy_eT(i, h - 1)
                    elif not first:
                        copy_eT(i - 1, H - 1)
                        row_inverse(i - 1, 1 - b)
                if not first:
                    scale_xc(i - 1, 1 - b)
                    stats_xc(i - 1)

            dve.wait_ge(xw_copied, 2 * T)
            head_max(0, 0, 0)
            tile_d(0, 0, first=True)
            tile_d(1, 1)
            tile_d(2, 0)
            with dve.Fori(3, T - 1, 2) as i:
                tile_d(i, 1)
                tile_d(i + 1, 0)
            tile_d(T - 1, 1, last=True)
            copy_eT(T - 1, H - 1)
            row_inverse(T - 1, 1)
            copy_rb(T - 1, 1)
            scale_xc(T - 1, 1)
            stats_xc(T - 1)

            def bn_affine(n, parts, gamma, beta):
                for c in range(KC):
                    dve.bn_aggr(bnmv[:, c], bnst[:, c, 0:parts].rearrange("p t s -> p (t s)")
                                ).then_inc(bn_mv, 1)
                dve.wait_ge(bn_mv, KC * (n + 1))
                dve.tensor_scalar(bnve[:], bnmv[:, :, 1], BN_EPS, None, ALU.add).then_inc(bn_ve, 1)
                dve.wait_ge(bn_rs, n + 1)
                dve.tensor_tensor(bna[:], vec[:, gamma], bnrs[:], ALU.mult).then_inc(bn_a, 1)
                dve.wait_ge(bn_a, n + 1)
                dve.tensor_tensor(bnt[:], bnmv[:, :, 0], bna[:], ALU.mult).then_inc(bn_t, 1)
                dve.wait_ge(bn_t, n + 1)
                dve.tensor_tensor(bnb[:], vec[:, beta], bnt[:], ALU.subtract).then_inc(bn_b, 1)
                dve.wait_ge(bn_b, n + 1)

            def affine0(buf, done):
                for c in range(NCH):
                    cs = slice(c * CH, (c + 1) * CH)
                    dve.tensor_scalar(buf[:, 0, cs], buf[:, 0, cs], bna[:, 0:1], bnb[:, 0:1], ALU.mult,
                                      ALU.add).then_inc(done, 1)

            dve.wait_ge(xc_stats, KC * T)
            bn_affine(0, T, ENC_G, ENC_B)
            affine0(xc, xn0_ready)

            def stats_hb(n):
                f, c = n % KC, n // KC
                dve.wait_ge(hb_ready, n + 1)
                dve.bn_stats(bnst[:, f, c], hb[:, f, c * CH:(c + 1) * CH]).then_inc(hb_stats, 1)

            for n in range(KC * NCH):
                f, c = n % KC, n // KC
                cs = slice(c * CH, (c + 1) * CH)
                dve.wait_ge(z_exp, n + 1)
                if f == 0:
                    dve.wait_ge(xn0_ready, c + 1)
                else:
                    dve.wait_ge(xn1_ready, c + 1)
                dve.scalar_tensor_tensor(et[:, 4 + n % 2], et[:, n % 2], 1.0, xc[:, f, cs], ALU.min, ALU.add
                                         ).then_inc(z_t, 1)
                if n > 0:
                    stats_hb(n - 1)
                dve.wait_ge(z_relu, n + 1)
                dve.wait_ge(z_t, n + 1)
                dve.scalar_tensor_tensor(hb[:, f, cs], et[:, 2 + n % 2], -1.0, et[:, 4 + n % 2], ALU.add,
                                         ALU.add).then_inc(hb_ready, 1)
            stats_hb(KC * NCH - 1)
            dve.wait_ge(hb_stats, KC * NCH)
            bn_affine(1, NCH, EMLP_G, EMLP_BETA)

            def scale_y(n, tile, c):
                wait(dve, yt_ready, KC * (n - 1) + c + 1)
                dve.tensor_scalar(yb[:, c], rb[:, c, tile_cols(tile)], 0.0, bnb[:, c:c + 1], ALU.is_gt, ALU.mult
                                  ).then_inc(yb_ready, 1)
                dve.wait_ge(y_done, KC * n + c + 1)
                wait(dve, yw_done, n)
                dve.tensor_tensor(yt[:, c], bank[c][:, 0:P], rb[:, c, tile_cols(tile)], ALU.mult
                                  ).then_inc(ys_ready, 1)
                dve.wait_ge(yb_ready, KC * n + c + 1)
                dve.wait_ge(ys_ready, KC * n + c + 1)
                dve.scalar_tensor_tensor(yt[:, c], yt[:, c], bna[:, c:c + 1], yb[:, c], ALU.mult, ALU.add
                                         ).then_inc(yt_ready, 1)

            def elu(n):
                dve.wait_ge(e1_ready, n + 1)
                dve.tensor_scalar(e1, e1, 1.0, -1.0, ALU.min, ALU.add).then_inc(t1_ready, 1)
                wait(dve, zd_done, n)
                dve.wait_ge(t1_ready, n + 1)
                dve.scalar_tensor_tensor(yc, bank[2][:, 0:D].rearrange("p (c n) -> p c n", c=KC), 0.0,
                                         e1, ALU.max, ALU.add).then_inc(yc_ready, 1)

            def mlp_in(n):
                dve.wait_ge(zd_exp, KC * (n + 1))
                dve.scalar_tensor_tensor(e2, e2, 1.0, yc, ALU.min, ALU.add).then_inc(t2_ready, 1)

            def mlp_out(n, tile):
                dve.wait_ge(zd_relu, KC * (n + 1))
                dve.wait_ge(t2_ready, n + 1)
                dve.scalar_tensor_tensor(hd[:, :, tile_cols(tile)], r2, -1.0, e2, ALU.add, ALU.add
                                         ).then_inc(hd_ready, 1)
                dve.wait_ge(hd_ready, n + 1)
                for c in range(KC):
                    dve.bn_stats(bnst[:, c, tile_row(tile)].rearrange("p o s -> p (o s)"),
                                 hd[:, c, tile_cols(tile)]).then_inc(hd_stats, 1)

            scale_y(0, T - 1, 0)
            scale_y(0, T - 1, 1)

            def step_f(n, tile, before):
                scale_y(n, tile, 0)
                elu(n - 1)
                scale_y(n, tile, 1)
                mlp_in(n - 1)
                mlp_out(n - 1, before)

            step_f(1, 0, T - 1)
            step_f(2, 1, 0)
            step_f(3, 2, 1)
            with dve.Fori(1, T // 4) as r:
                for b in range(4):
                    step_f(4 * r + b, 4 * r + b - 1, 4 * r + b - 2)
            elu(T - 1)
            mlp_in(T - 1)
            mlp_out(T - 1, T - 2)

            dve.wait_ge(hd_stats, KC * T)
            bn_affine(2, T, DMLP_G, DMLP_BETA)
            affine0(hd, hdn0_ready)
            for n in range(T // 2):
                dve.wait_ge(oT_filled, n + 1)
                dve.tensor_tensor(ob[:, 2 * n:2 * n + 2], bank[4 + n % 4][:].rearrange("p (t d) -> p t d", t=2),
                                  x_sb[:, 2 * n:2 * n + 2], ALU.add).then_inc(o_ready, 1)


def kernel(**inputs):
    import numpy as np
    import concourse.bacc as bacc
    from concourse.bass_utils import run_bass_kernel_spmd

    a = {k: np.asarray(v) for k, v in inputs.items()}
    names = ["L0_gnn_bq", "L0_gnn_bk", "L1_gnn_enc_bn_gamma", "L1_gnn_enc_bn_beta", "L1_gnn_enc_mlp_b",
             "L1_gnn_enc_mlp_bn_gamma", "L1_gnn_enc_mlp_bn_beta", "L1_gnn_dec_mlp_b",
             "L1_gnn_dec_mlp_bn_gamma", "L1_gnn_dec_mlp_bn_beta"]
    arrays = {
        "x": a["x"],
        "adj": a["adj"],
        "wqT": a["L0_gnn_Wq"].T,
        "wkT": a["L0_gnn_Wk"].T,
        "wvT": a["L0_gnn_Wv"].T,
        "bv": a["L0_gnn_bv"],
        "cols": np.stack([a[n] for n in names]).reshape(len(names), -1, P).transpose(2, 0, 1),
        "w_head": a["L1_gnn_W"],
        "w_headT": a["L1_gnn_W"].transpose(0, 2, 1),
        "v_head": a["L1_gnn_V"][..., 0].transpose(0, 2, 1),
        "enc_wT": a["L1_gnn_enc_mlp_W"].T,
        "dec_wT": a["L1_gnn_dec_mlp_W"].T,
    }
    arrays = {f"in_{k}": np.ascontiguousarray(v) for k, v in arrays.items()}
    nc = bacc.Bacc("TRN2", target_bir_lowering=False, num_devices=1, dynamic_dma_scratch_size=KIB)
    args = [nc.dram_tensor(k, v.shape, mybir.dt.from_np(v.dtype), kind="ExternalInput").ap()
            for k, v in arrays.items()]
    out = nc.dram_tensor("out", a["x"].shape, mybir.dt.from_np(a["x"].dtype), kind="ExternalOutput").ap()
    build(nc, *args, out)
    r = run_bass_kernel_spmd(nc, [arrays], core_ids=[0])
    return r.results[0]["out"]
```
